# Optimizing a Trainium2 kernel written in Bass

```python
import numpy as np
import jax
import jax.numpy as jnp

def _softmax(x, axis=-1):
    return jax.nn.softmax(x, axis=axis)

def _gelu(x):
    return jax.nn.gelu(x, approximate=True)

def _silu(x):
    return jax.nn.silu(x)

def _sigmoid(x):
    return jax.nn.sigmoid(x)

def _layernorm(x, axis=-1, eps=1e-05):
    m = jnp.mean(x, axis=axis, keepdims=True)
    v = jnp.var(x, axis=axis, keepdims=True)
    return (x - m) / jnp.sqrt(v + eps)

def _scatter_add(tgt, idx, src, axis=0):
    return tgt.at[idx].add(src)

def _segment_sum(src, seg, n):
    return jax.ops.segment_sum(src, seg, n)
kernel_name = 'mk_xattn_ffn_d1_seqx_r4_6728f7'

def setup_inputs(seed: int=0):
    np.random.seed(seed)
    _w = jnp.asarray

    def _rec_inputs():
        import jax
        import jax.numpy as jnp
        _rk = jax.random.key(seed)
        x = -0.0003929 + 0.9999 * jax.random.normal(jax.random.fold_in(_rk, 1), (4, 1024, 256), jnp.float32)
        _lenS = 1024 - jax.random.randint(jax.random.fold_in(_rk, 7), (4,), 0, max(1, 1024 // 4) + 1, jnp.int32)
        _lenS2 = 64 - jax.random.randint(jax.random.fold_in(_rk, 8), (4,), 0, max(1, 64 // 4) + 1, jnp.int32)
        _ctx_1024P = jax.random.normal(jax.random.fold_in(_rk, 11), (4, 16, 256), jnp.float32)
        _ctx_1024c = jax.random.dirichlet(jax.random.fold_in(_rk, 511), 0.3 * jnp.ones((16,), jnp.float32), (4, 64))
        _ctx_1024t = jnp.einsum('bsk,bkd->bsd', _ctx_1024c, _ctx_1024P)
        _ctx_1024t = _ctx_1024t * jax.lax.rsqrt(jnp.mean(jnp.square(_ctx_1024t)) + 1e-12) * 0.953939
        ctx_1024 = 2.81802e-05 + 1.00001 * (_ctx_1024t + 0.3 * jax.random.normal(jax.random.fold_in(_rk, 611), (4, 64, 256), jnp.float32))
        return (x, ctx_1024)
    x, ctx_1024 = _rec_inputs()

    def _L0_xattn_setup():
        import jax, jax.numpy as jnp
        import numpy as np
        B, SQ, SKV, D = (8, 512, 512, 256)
        key = jax.random.key(seed)
        ks = jax.random.split(key, 8)
        s = 1.0 / np.sqrt(D)
        return {'target': jax.random.normal(ks[0], (B, SQ, D), dtype=jnp.float32), 'non_target': jax.random.normal(ks[1], (B, SKV, D), dtype=jnp.float32), 'Wq': jax.random.uniform(ks[2], (D, D), jnp.float32, -s, s), 'bq': jax.random.uniform(ks[3], (D,), jnp.float32, -s, s), 'Wk': jax.random.uniform(ks[4], (D, D), jnp.float32, -s, s), 'bk': jax.random.uniform(ks[5], (D,), jnp.float32, -s, s), 'Wv': jax.random.uniform(ks[6], (D, D), jnp.float32, -s, s), 'bv': jax.random.uniform(ks[7], (D,), jnp.float32, -s, s)}
    _L0_xattn_all = _L0_xattn_setup()
    _L0_xattn_in = {k: v for k, v in _L0_xattn_all.items() if k in ('Wq', 'bq', 'Wk', 'bk', 'Wv', 'bv')}
    del _L0_xattn_all

    def _L0_ffn_setup():
        import jax, jax.numpy as jnp
        import numpy as np
        NUM_EXPERTS = 8
        EXPERT_CAPACITY = 2.0
        key = jax.random.key(seed)
        k1, k2, k3, k4 = jax.random.split(key, 4)
        B, T, C, H, E = (4, 1024, 256, 1024, NUM_EXPERTS)
        x = jax.random.normal(k1, (B, T, C), jnp.float32)
        gate_w = jax.random.normal(k2, (C, E), jnp.float32) * 0.02
        w1 = jax.random.normal(k3, (E, C, H), jnp.float32) * 0.02
        w2 = jax.random.normal(k4, (E, H, C), jnp.float32) * 0.02
        return {'x': x, 'gate_w': gate_w, 'w1': w1, 'w2': w2}
    _L0_ffn_all = _L0_ffn_setup()
    _L0_ffn_in = {k: v for k, v in _L0_ffn_all.items() if k in ('gate_w', 'w1', 'w2')}
    del _L0_ffn_all
    return {'x': x, 'ctx_1024': ctx_1024, 'L0_xattn_Wq': _L0_xattn_in['Wq'], 'L0_xattn_bq': _L0_xattn_in['bq'], 'L0_xattn_Wk': _L0_xattn_in['Wk'], 'L0_xattn_bk': _L0_xattn_in['bk'], 'L0_xattn_Wv': _L0_xattn_in['Wv'], 'L0_xattn_bv': _L0_xattn_in['bv'], 'L0_ffn_gate_w': _L0_ffn_in['gate_w'], 'L0_ffn_w1': _L0_ffn_in['w1'], 'L0_ffn_w2': _L0_ffn_in['w2']}

def reference(x, ctx_1024, L0_xattn_Wq, L0_xattn_bq, L0_xattn_Wk, L0_xattn_bk, L0_xattn_Wv, L0_xattn_bv, L0_ffn_gate_w, L0_ffn_w1, L0_ffn_w2):
    import jax
    import jax.numpy as jnp

    def _L0_xattn_ref(target, non_target, Wq, bq, Wk, bk, Wv, bv):
        import jax, jax.numpy as jnp
        import numpy as np
        B, SQ, SKV, D = (8, 512, 512, 256)
        q = jnp.einsum('bsd,ed->bse', target, Wq) + bq
        k = jnp.einsum('bsd,ed->bse', non_target, Wk) + bk
        v = jnp.einsum('bsd,ed->bse', non_target, Wv) + bv
        scores = jnp.einsum('bqd,bkd->bqk', q, k)
        weights = jax.nn.softmax(scores, axis=-1)
        return jnp.einsum('bqk,bkd->bqd', weights, v)

    def _L0_ffn_ref(x, gate_w, w1, w2):
        import jax, jax.numpy as jnp
        import numpy as np
        NUM_EXPERTS = 8
        EXPERT_CAPACITY = 2.0
        B, T, C = x.shape
        E = gate_w.shape[1]
        cap = int(EXPERT_CAPACITY * T / E)
        scores = jnp.einsum('BTC,CE->BTE', x, gate_w)
        probs = jax.nn.softmax(scores, axis=-1)
        probs_et = jnp.transpose(probs, (0, 2, 1))
        top_p, top_idx = jax.lax.top_k(probs_et, cap)
        xin = jnp.take_along_axis(x[:, None, :, :], top_idx[..., None], axis=2)
        h = jax.nn.gelu(jnp.einsum('BElC,ECH->BElH', xin, w1), approximate=False)
        y = jnp.einsum('BElH,EHC->BElC', h, w2)
        y = y * top_p[..., None]
        b_idx = jnp.arange(B)[:, None, None]
        out = jnp.zeros((B, T, C), x.dtype).at[b_idx, top_idx].add(y)
        return out
    x = x + _L0_xattn_ref(_layernorm(x, axis=-1), ctx_1024, L0_xattn_Wq, L0_xattn_bq, L0_xattn_Wk, L0_xattn_bk, L0_xattn_Wv, L0_xattn_bv)
    x = x + _L0_ffn_ref(_layernorm(x, axis=-1), L0_ffn_gate_w, L0_ffn_w1, L0_ffn_w2)
    return x

_drawn_inputs = setup_inputs


def setup_inputs(seed=0):
    import zlib

    import numpy as np

    out = dict(_drawn_inputs(seed))
    spreads = {}
    factors = {'L0_xattn_bk': 8.0, 'L0_ffn_gate_w': 2.686}
    for name, (base, spread) in spreads.items():
        noise = np.random.default_rng([zlib.crc32(name.encode()), seed]).standard_normal(out[name].shape)
        drawn = base * np.exp(spread * noise) if base else spread * noise
        out[name] = jnp.asarray(drawn.astype(out[name].dtype))
    for name, factor in factors.items():
        out[name] = (out[name] * factor).astype(out[name].dtype)
    return out
```

```python
from contextlib import ExitStack

import concourse.bass as bass
from concourse import mybir

F32 = mybir.dt.float32
F32R = mybir.dt.float32r
BF16 = mybir.dt.bfloat16
F16 = mybir.dt.float16
I32 = mybir.dt.int32
ALU = mybir.AluOpType
ACT = mybir.ActivationFunctionType
AX = mybir.AxisListType

P = 128
EPS = 1e-5


def wait_count(eng, sem, n):
    if isinstance(n, int) and n <= 0:
        return
    eng.wait_ge(sem, n)


def build(nc, x, ctx_in, Wq, bq, Wk, bk, Wv, bv, gate_w, w1, w2, out):
    B, T, C = x.shape
    S = ctx_in.shape[1]
    E, _, H = w1.shape
    CAP = 2 * T // E
    TC = T // P
    NC = B * TC
    KC = C // P
    HC = H // P
    GT = 4
    NG = NC // GT
    GB = TC // GT
    LB = CAP // P
    UB = 2
    NU = B // UB
    NL = UB * LB
    UT = NL * P
    ST = NU * HC
    BITS, RB = 30, 2
    KT = 2 ** RB - 1
    ROUNDS = BITS // RB
    assert KC == 2 and UT == 512 and B * S == 2 * P and NC * E == 256

    xn_dram = nc.dram_tensor("xn_rows", (B * T, C), F32, kind="Internal").ap()
    pr_dram = nc.dram_tensor("prob_rows", (B * T, E), F32, kind="Internal").ap()

    x_v = x.rearrange("b (p c) d -> b p c d", c=TC)
    out_v = out.rearrange("b (p c) d -> p b c d", c=TC)
    xn_v = xn_dram.rearrange("(b p c) d -> p b c d", b=B, c=TC)
    pr_v = pr_dram.rearrange("(b p c) e -> p b (c e)", b=B, c=TC)
    out_rows = out.rearrange("b t d -> (b t) d")

    with ExitStack() as stack:
        def sb(name, shape, dt):
            return stack.enter_context(nc.sbuf_tensor(name, shape, dt))

        def sem(name):
            return stack.enter_context(nc.semaphore(name))

        bank = [stack.enter_context(nc.psum_tensor(f"bank{i}", [P, 512], F32)) for i in range(8)]

        identf = sb("identf", [P, P], F32)
        identb = sb("identb", [P, P], BF16)
        onesb = sb("onesb", [P, P], BF16)
        before = sb("before", [P, P], BF16)
        ones_row = sb("ones_row", [1, P], F32)
        slot_no = sb("slot_no", [P, P], F16)
        tok_no = sb("tok_no", [P, B, TC, E], F32)
        row0 = sb("row0", [P, B * LB], F32)
        neghalf = sb("neghalf", [P, GT], F32)
        cand_off = sb("cand_off", [P, B, KT, E], I32)
        bit_step = sb("bit_step", [P, 1], F32)
        wk_sb = sb("wk_sb", [P, KC, C], F32)
        wq_sb = sb("wq_sb", [P, KC, C], F32)
        wv_sb = sb("wv_sb", [P, KC, C], F32)
        ctx_sb = sb("ctx_sb", [P, KC, C], F32)
        bk_sb = sb("bk_sb", [P, KC], F32)
        bq_sb = sb("bq_sb", [P, KC], F32)
        bv_row = sb("bv_row", [1, C], F32)
        gate_sb = sb("gate_sb", [P, KC, E], F32)
        ctxT = sb("ctxT", [P, KC, B * S], F32)
        wkT = sb("wkT", [P, KC, C], F32)
        wvT = sb("wvT", [P, KC, C], F32)
        kT = sb("kT", [P, KC, B * S], F32)
        qk = sb("qk", [P, KC, B * S], F32)
        qk_bias = sb("qk_bias", [1, B * S], F32)
        v_sb = sb("v_sb", [S, B, C], F32)
        x_all = sb("x_all", [P, B, TC, C], F32)
        st1 = sb("st1", [P, GT, 6], F32)
        mv1 = sb("mv1", [P, GT, 2], F32)
        ve1 = sb("ve1", [P, GT], F32)
        rs1 = sb("rs1", [P, GT], F32)
        xn1 = sb("xn1", [P, GT, C], F32)
        xn1T = sb("xn1T", [P, KC, GT * P], F32)
        nmax = sb("nmax", [P, GT], F32)
        prb = sb("prb", [P, GT, S], F32)
        psums = sb("psums", [P, GT], F32)
        prbT = sb("prbT", [S, GT * P], F32)
        rinv = sb("rinv", [P, GT], F32)
        st2 = sb("st2", [P, GT, 6], F32)
        mv2 = sb("mv2", [P, GT, 2], F32)
        ve2 = sb("ve2", [P, GT], F32)
        rs2 = sb("rs2", [P, GT], F32)
        xn2 = sb("xn2", [P, GT, C], F32)
        xn2T = sb("xn2T", [P, KC, GT * P], F32)
        gmax = sb("gmax", [P, NC], F32)
        gsum = sb("gsum", [P, NC], F32)
        prob = sb("prob", [P, B, TC, E], F32)
        floor_ = sb("floor", [P, B, E], I32)
        cand = sb("cand", [P, B, KT, E], I32)
        over = sb("over", [P, B, TC, KT * E], BF16)
        enough = sb("enough", [P, B, KT, E], F32)
        gain = sb("gain", [P, B, E], I32)
        above = sb("above", [P, B, TC, E], BF16)
        tied = sb("tied", [P, B, TC, E], BF16)
        pos_a = sb("pos_a", [P, B, TC, E], F32)
        pos_t = sb("pos_t", [P, B, TC, E], F32)
        second = sb("second", [P, B, TC, E], F32)
        slot_of = sb("slot_of", [P, B * TC, E], F32)
        tok_val = sb("tok_val", [P, B * TC, E, LB], F16)
        slot_e = sb("slot_e", [P, B * TC], F32)
        val_e = sb("val_e", [P, B * TC, LB], F16)
        onehot = sb("onehot", [P, B * TC, P], F16)
        gidx = sb("gidx", [P, B * LB], I32)
        sidx = sb("sidx", [P, B * LB], I32)
        w1raw = sb("w1raw", [P, KC, H], F32)
        w2raw = sb("w2raw", [P, HC, C], F32)
        w1hi = sb("w1hi", [P, HC, KC, P], F32R)
        w1lo = sb("w1lo", [P, HC, KC, P], F32R)
        w2hi = sb("w2hi", [P, HC, C], F32R)
        w2lo = sb("w2lo", [P, HC, C], F32R)
        xg = [sb(f"xg{g}", [P, NL, C], F32) for g in range(NU)]
        pg = [sb(f"pg{g}", [P, NL, E], F32) for g in range(NU)]
        pcol = [sb(f"pcol{g}", [P, NL], F32) for g in range(NU)]
        xhi = [sb(f"xhi{g}", [P, KC, UT], F32R) for g in range(NU)]
        xlo = [sb(f"xlo{g}", [P, KC, UT], F32R) for g in range(NU)]
        hraw = [sb(f"hraw{i}", [P, UT], F32) for i in range(2)]
        hhi = [sb(f"hhi{i}", [P, UT], F32R) for i in range(4)]
        hlo = [sb(f"hlo{i}", [P, UT], F32R) for i in range(4)]
        ysb = [sb(f"ysb{g}", [P, NL, C], F32) for g in range(NU)]

        kv_loaded = sem("kv_loaded")
        qv_loaded = sem("qv_loaded")
        x_first = sem("x_first")
        x_rest = sem("x_rest")
        consts = sem("consts")
        bits_set = sem("bits_set")
        folded = sem("folded")
        setup_out = sem("setup_out")
        stats1 = sem("stats1")
        var1 = sem("var1")
        rstd1 = sem("rstd1")
        xn1_ready = sem("xn1_ready")
        xn1_turned = sem("xn1_turned")
        xn1T_ready = sem("xn1T_ready")
        scored = sem("scored")
        max_ready = sem("max_ready")
        exp_done = sem("exp_done")
        prb_turned = sem("prb_turned")
        prbT_ready = sem("prbT_ready")
        attended = sem("attended")
        rinv_ready = sem("rinv_ready")
        x1_ready = sem("x1_ready")
        stats2 = sem("stats2")
        var2 = sem("var2")
        rstd2 = sem("rstd2")
        xn2_ready = sem("xn2_ready")
        xn2_turned = sem("xn2_turned")
        xn2T_ready = sem("xn2T_ready")
        gated = sem("gated")
        rows_stored = sem("rows_stored")
        rows_added = sem("rows_added")
        settled = sem("settled")
        xn_stored = sem("xn_stored")
        soft = sem("soft")
        gexp = sem("gexp")
        pr_stored = sem("pr_stored")
        cand_ready = sem("cand_ready")
        over_ready = sem("over_ready")
        counted = sem("counted")
        enough_ready = sem("enough_ready")
        gain_ready = sem("gain_ready")
        floor_ready = sem("floor_ready")
        step_ready = sem("step_ready")
        masks = sem("masks")
        ranked = sem("ranked")
        placed = sem("placed")
        col_ready = sem("col_ready")
        onehot_ready = sem("onehot_ready")
        listed = sem("listed")
        gidx_ready = sem("gidx_ready")
        sidx_ready = sem("sidx_ready")
        raw_loaded = sem("raw_loaded")
        w1_hi = sem("w1_hi")
        w2_hi = sem("w2_hi")
        first_split = sem("first_split")
        w1_split = sem("w1_split")
        w2_split = sem("w2_split")
        gathered = [sem(f"gathered{g}") for g in range(NU)]
        xg_turned = sem("xg_turned")
        x_hi = sem("x_hi")
        x_split = sem("x_split")
        pcol_ready = sem("pcol_ready")
        ff1_done = sem("ff1_done")
        gelu_done = sem("gelu_done")
        h_hi = sem("h_hi")
        h_split = sem("h_split")
        ff2_done = sem("ff2_done")
        y_ready = sem("y_ready")

        dve_passed = sem("dve_passed")
        pe_passed = sem("pe_passed")
        pool_passed = sem("pool_passed")

        def keep_wait(eng, passed):
            eng.sem_inc(passed, 1)

        N_FOLD = 7

        LAST = 3

        def active(j, stage):
            return not isinstance(j, int) or 0 <= j - stage < NG

        def run_steps(eng, body):
            for j in range(LAST):
                body(j)
            with eng.Fori(LAST, NG) as j:
                body(j)
            for j in range(NG, NG + LAST):
                body(j)

        def xcols(g):
            return x_all[:].rearrange("p b c d -> p (b c) d")[:, bass.ts(g, GT), :]

        def run_experts(eng, body):
            with eng.Fori(0, E - 1) as e:
                body(e, False)
            body(E - 1, True)

        block = stack.enter_context(nc.Block())

        @block.sync
        def _(sp):
            sp.dma_start(wk_sb[:], Wk.rearrange("(k p) d -> p k d", p=P)).then_inc(kv_loaded, 16)
            sp.dma_start(ctx_sb[:], ctx_in.rearrange("b s d -> (b s) d").rearrange("(k p) d -> p k d", p=P)).then_inc(kv_loaded, 16)
            sp.dma_start(x_all[:, 0], x_v[0]).then_inc(x_first, 16)
            sp.dma_start(bk_sb[:], bk.rearrange("(k p) -> p k", p=P), allow_slow_non_contiguous=True).then_inc(kv_loaded, 16)
            sp.dma_start(wq_sb[:], Wq.rearrange("(k p) d -> p k d", p=P)).then_inc(qv_loaded, 16)
            sp.dma_start(bq_sb[:], bq.rearrange("(k p) -> p k", p=P), allow_slow_non_contiguous=True).then_inc(qv_loaded, 16)
            sp.dma_start(bv_row[:], bv.rearrange("(a d) -> a d", a=1)).then_inc(qv_loaded, 16)
            sp.dma_start(wv_sb[:], Wv.rearrange("(k p) d -> p k d", p=P)).then_inc(qv_loaded, 16)
            sp.dma_start(gate_sb[:], gate_w.rearrange("(k p) e -> p k e", p=P)).then_inc(qv_loaded, 16)
            for b in range(1, B):
                sp.dma_start(x_all[:, b], x_v[b]).then_inc(x_rest, 16)
            sp.dma_start(w1raw[:], w1[0].rearrange("(k p) h -> p k h", p=P)).then_inc(raw_loaded, 16)
            sp.dma_start(w2raw[:], w2[0].rearrange("(k p) d -> p k d", p=P)).then_inc(raw_loaded, 16)

            out_g = out.rearrange("b (p q c) d -> p b q (c d)", q=GB, c=GT)
            xn_g = xn_dram.rearrange("(b p q c) d -> p b q (c d)", b=B, q=GB, c=GT)

            def step(j):
                if active(j, 2):
                    g = j - 2
                    sp.wait_ge(x1_ready, g + 1)
                    sp.dma_start(out_g[:, g // GB, g % GB], xcols(g)).then_inc(rows_stored, 16)
                if active(j, 3):
                    g = j - 3
                    sp.wait_ge(xn2_ready, g + 1)
                    sp.dma_start(xn_g[:, g // GB, g % GB], xn2[:]).then_inc(xn_stored, 16)

            run_steps(sp, step)
            sp.wait_ge(soft, 5)
            sp.dma_start(pr_v, prob[:].rearrange("p b c e -> p b (c e)")).then_inc(pr_stored, 16)

            def load_next(e, last):
                if not last:
                    sp.wait_ge(w2_split, HC * (e + 1))
                    sp.dma_start(w1raw[:], w1_v[:, e + 1]).then_inc(raw_loaded, 16)
                    sp.dma_start(w2raw[:], w2_v[:, e + 1]).then_inc(raw_loaded, 16)

            w1_v = w1.rearrange("e (k p) h -> p e k h", p=P)
            w2_v = w2.rearrange("e (k p) d -> p e k d", p=P)
            run_experts(sp, load_next)

        @block.gpsimd
        def _(pool):
            pool.memset(identf[:], 0.0).then_inc(bits_set, 1)
            pool.memset(identb[:], 0.0).then_inc(bits_set, 1)
            pool.memset(before[:], 1.0).then_inc(bits_set, 1)
            pool.memset(ones_row[:], 1.0).then_inc(consts, 1)
            pool.memset(neghalf[:], -0.5).then_inc(consts, 1)
            pool.wait_ge(bits_set, 3)
            for m in (identf, identb):
                pool.affine_select(out=m[:], in_=m[:], compare_op=ALU.not_equal, fill=1.0, base=0,
                                   pattern=[[-1, P]], channel_multiplier=1).then_inc(consts, 1)
            pool.affine_select(out=before[:], in_=before[:], compare_op=ALU.is_gt, fill=0.0, base=0,
                               pattern=[[1, P]], channel_multiplier=-1).then_inc(consts, 1)
            pool.memset(onesb[:], 1.0).then_inc(consts, 1)
            pool.memset(floor_[:], 0).then_inc(consts, 1)
            pool.memset(bit_step[:], float(2 ** (BITS - RB))).then_inc(consts, 1)
            pool.iota(cand_off[:], [[0, B], [1, KT], [0, E]], base=1, channel_multiplier=0).then_inc(consts, 1)
            pool.iota(slot_no[:], [[1, P]], base=1, channel_multiplier=0,
                      allow_small_or_imprecise_dtypes=True).then_inc(consts, 1)
            pool.iota(tok_no[:], [[0, B], [1, TC], [0, E]], base=0, channel_multiplier=TC,
                      allow_small_or_imprecise_dtypes=True).then_inc(consts, 1)
            pool.iota(row0[:], [[T, B], [0, LB]], base=0, channel_multiplier=0,
                      allow_small_or_imprecise_dtypes=True).then_inc(consts, 1)

            pool.wait_ge(consts, 2)

            def step(j):
                if active(j, 2):
                    g = j - 2
                    pool.wait_ge(var2, g + 1)
                    wait_count(pool, xn2_ready, g)
                    pool.tensor_tensor(rs2[:], ve2[:], neghalf[:], ALU.pow).then_inc(rstd2, 1)
                if active(j, 0):
                    g = j
                    pool.wait_ge(var1, g + 1)
                    wait_count(pool, xn1_ready, g)
                    pool.tensor_tensor(rs1[:], ve1[:], neghalf[:], ALU.pow).then_inc(rstd1, 1)

            run_steps(pool, step)

            for j in range(HC):
                pool.wait_ge(w1_hi, j + 1)
                pool.tensor_tensor(w1lo[:, j], w1raw[:, :, bass.ts(j, P)], w1hi[:, j].bitcast(F32),
                                   ALU.subtract).then_inc(first_split, 1)
            for j in range(HC - 1):
                pool.wait_ge(w2_hi, j + 1)
                pool.tensor_tensor(w2lo[:, j], w2raw[:, j], w2hi[:, j].bitcast(F32),
                                   ALU.subtract).then_inc(first_split, 1)

            def gather(g, e):
                keep_wait(pool, pool_passed)
                for i in range(NL):
                    at = bass.IndirectOffsetOnAxis(ap=gidx[:, g * NL + i:g * NL + i + 1], axis=0)
                    pool.indirect_dma_start(out=xg[g][:, i, :], out_offset=None, in_=xn_dram,
                                            in_offset=at).then_inc(gathered[g], 16)
                for i in range(NL):
                    at = bass.IndirectOffsetOnAxis(ap=gidx[:, g * NL + i:g * NL + i + 1], axis=0)
                    pool.indirect_dma_start(out=pg[g][:, i, :], out_offset=None, in_=pr_dram,
                                            in_offset=at).then_inc(gathered[g], 16)

            def scatter(g):
                keep_wait(pool, pool_passed)
                for i in range(NL):
                    at = bass.IndirectOffsetOnAxis(ap=sidx[:, g * NL + i:g * NL + i + 1], axis=0)
                    pool.indirect_dma_start(out=out_rows, out_offset=at, in_=ysb[g][:, i, :], in_offset=None,
                                            compute_op=ALU.add).then_inc(rows_added, 16)

            pool.wait_ge(xn_stored, 16 * NG)
            pool.wait_ge(pr_stored, 16)
            pool.wait_ge(gidx_ready, 1)
            gather(0, 0)
            gather(1, 0)

            def expert(e, last):
                if not last:
                    pool.wait_ge(gidx_ready, e + 2)
                    pool.wait_ge(xg_turned, 2 * NU * e + 4)
                    gather(0, e + 1)
                pool.wait_ge(sidx_ready, e + 1)
                pool.wait_ge(y_ready, 2 * e + 1)
                scatter(0)
                if not last:
                    pool.wait_ge(pcol_ready, 2 * e + 2)
                    gather(1, e + 1)
                pool.wait_ge(y_ready, 2 * e + 2)
                scatter(1)
                pool.wait_ge(rows_added, 16 * NU * NL * (e + 1))
                pool.sem_inc(settled, 1)

            pool.wait_ge(rows_stored, 16 * NG)
            pool.sem_inc(settled, 1)
            run_experts(pool, expert)

        @block.scalar
        def _(act):
            def evac(dst, src, n, **kw):
                act.wait_ge(folded, n)
                act.activation(dst, src, ACT.Identity if kw else ACT.Copy, **kw).then_inc(setup_out, 1)

            evac(ctxT[:].rearrange("p k s -> p (k s)"), bank[0][:], 1)
            evac(wkT[:].rearrange("p k s -> p (k s)"), bank[1][:], 2)
            act.wait_ge(kv_loaded, 48)
            act.wait_ge(folded, 3)
            act.activation(kT[:, 0], bank[3][:, 0:256], ACT.Identity, bias=bk_sb[:, 0:1])
            act.activation(kT[:, 1], bank[3][:, 256:512], ACT.Identity, bias=bk_sb[:, 1:2]).then_inc(setup_out, 1)
            evac(wvT[:].rearrange("p k s -> p (k s)"), bank[2][:], 4)
            evac(qk[:].rearrange("p k s -> p (k s)"), bank[7][:], 5)
            evac(qk_bias[:], bank[6][0:1, 0:B * S], 6)
            act.wait_ge(folded, 7)
            act.activation(v_sb[:, 0:2].rearrange("p b d -> p (b d)"), bank[4][0:S, :], ACT.Copy)
            act.activation(v_sb[:, 2:4].rearrange("p b d -> p (b d)"), bank[5][0:S, :], ACT.Copy).then_inc(setup_out, 1)

            def step(j):
                if active(j, 2):
                    g = j - 2
                    act.wait_ge(prb_turned, g + 1)
                    act.activation(prbT[:], bank[3][0:S, :], ACT.Copy).then_inc(prbT_ready, 1)
                if active(j, 3):
                    g = j - 3
                    for k in range(KC):
                        act.wait_ge(xn2_turned, KC * g + k + 1)
                        act.activation(xn2T[:, k], bank[k][:], ACT.Copy).then_inc(xn2T_ready, 1)
                if active(j, 1):
                    g = j - 1
                    for k in range(KC):
                        act.wait_ge(xn1_turned, KC * g + k + 1)
                        act.activation(xn1T[:, k], bank[k][:], ACT.Copy).then_inc(xn1T_ready, 1)
                    act.wait_ge(max_ready, g + 1)
                    for i in range(GT):
                        a = act.activation(prb[:, i, :], bank[2][:, i * S:(i + 1) * S], ACT.Exp,
                                           bias=nmax[:, i:i + 1], accum_out=psums[:, i:i + 1])
                    a.then_inc(exp_done, 1)

            run_steps(act, step)

            act.wait_ge(soft, 2)
            pr = prob[:].rearrange("p b c e -> p (b c e)")
            act.activation(pr, pr, ACT.Exp).then_inc(gexp, 1)

            def w1_part(j, n):
                act.activation(w1hi[:, j], w1raw[:, :, bass.ts(j, P)], ACT.Copy).then_inc(w1_hi, 1)

            def w2_part(j, n):
                act.activation(w2hi[:, j], w2raw[:, j], ACT.Copy).then_inc(w2_hi, 1)

            act.wait_ge(raw_loaded, 32)
            for j in range(HC):
                w1_part(j, 0)
            for j in range(HC - 1):
                w2_part(j, 0)

            def x_part(g, k, n):
                act.wait_ge(xg_turned, n)
                act.activation(xhi[g][:, k], bank[2][:], ACT.Copy).then_inc(x_hi, 1)

            def gelu(s, n):
                act.wait_ge(ff1_done, n + 1)
                if not (isinstance(n, int) and n < 2):
                    act.wait_ge(h_split, n - 1)
                act.activation(hraw[s % 2][:], bank[s % 2][:], ACT.Gelu).then_inc(gelu_done, 1)

            def y_rows(g, e):
                act.wait_ge(ff2_done, ST * e + HC * (g + 1))
                act.wait_ge(pcol_ready, 2 * e + g + 1)
                if g == 0:
                    act.wait_ge(settled, e + 1)

                for i in range(NL):
                    a = act.activation(ysb[g][:, i, :], bank[4 + 2 * g + i // 2][:, (i % 2) * C:(i % 2 + 1) * C],
                                       ACT.Copy, scale=pcol[g][:, i:i + 1])
                a.then_inc(y_ready, 1)

            for k in range(KC):
                x_part(0, k, k + 1)
            gelu(0, 0)
            gelu(1, 1)

            def expert(e, last):
                for s in range(ST):
                    if s in (1, 2):
                        x_part(1, s - 1, 2 * NU * e + 2 + s)
                    if s in (10, 11) and not last:
                        x_part(0, s - 10, 2 * NU * (e + 1) + s - 9)
                    if s == 0:
                        act.wait_ge(ff1_done, ST * e + 2)
                        w2_part(HC - 1, 0)
                    if s == HC - 1 and not last:
                        act.wait_ge(raw_loaded, 32 * (e + 2))
                    if HC - 1 <= s < 2 * HC - 1 and not last:
                        j = s - (HC - 1)
                        act.wait_ge(ff1_done, ST * e + HC + j + 1)
                        w1_part(j, 0)
                    if s > HC and not last:
                        j = s - HC - 1
                        act.wait_ge(ff2_done, ST * e + HC + j + 1)
                        w2_part(j, 0)
                    if s + 2 < ST or not last:
                        gelu(s + 2, ST * e + s + 2)
                    if s % HC == HC - 1:
                        y_rows(s // HC, e)

            run_experts(act, expert)

        @block.tensor
        def _(pe):
            def turn(dst, src, ident=identf):
                return pe.transpose(dst, src, ident[:])

            pe.wait_ge(consts, 5)
            pe.wait_ge(kv_loaded, 48)
            for dst, src in ((bank[0], ctx_sb), (bank[1], wk_sb)):
                for k in range(KC):
                    for r in range(2):
                        t = turn(dst[:, k * 256 + r * P:k * 256 + (r + 1) * P], src[:, r, k * P:(k + 1) * P])
                t.then_inc(folded, 1)
            pe.wait_ge(setup_out, 2)
            for m in range(KC):
                for k in range(KC):
                    t = pe.matmul(bank[3][:, m * 256:(m + 1) * 256], wkT[:, k, m * P:(m + 1) * P], ctxT[:, k, :],
                                  start=(k == 0), stop=(k == KC - 1))
            t.then_inc(folded, 1)
            pe.wait_ge(qv_loaded, 80)
            for k in range(KC):
                for r in range(2):
                    t = turn(bank[2][:, k * 256 + r * P:k * 256 + (r + 1) * P], wv_sb[:, r, k * P:(k + 1) * P])
            t.then_inc(folded, 1)
            pe.wait_ge(setup_out, 3)
            for m in range(KC):
                for k in range(KC):
                    t = pe.matmul(bank[7][:, m * 256:(m + 1) * 256], wq_sb[:, k, m * P:(m + 1) * P], kT[:, k, :],
                                  start=(k == 0), stop=(k == KC - 1))
            t.then_inc(folded, 1)
            for k in range(KC):
                t = pe.matmul(bank[6][0:1, 0:B * S], bq_sb[:, k:k + 1], kT[:, k, :], start=(k == 0), stop=(k == KC - 1))
            t.then_inc(folded, 1)
            pe.wait_ge(setup_out, 4)
            for b in range(B):
                o = bank[4 + b // 2][0:S, (b % 2) * C:(b % 2 + 1) * C]
                for k in range(KC):
                    pe.matmul(o, ctxT[:, k, b * S:(b + 1) * S], wvT[:, k, :], start=(k == 0), stop=False)
                t = pe.matmul(o, ones_row[:, 0:S], bv_row[:], start=False, stop=True)
            t.then_inc(folded, 1)
            pe.wait_ge(setup_out, N_FOLD)

            def step(j):
                if active(j, 2):
                    g = j - 2
                    pe.wait_ge(exp_done, g + 1)
                    wait_count(pe, prbT_ready, g)
                    keep_wait(pe, pe_passed)
                    for i in range(GT):
                        t = turn(bank[3][0:S, i * P:(i + 1) * P], prb[:, i, :])
                    t.then_inc(prb_turned, 1)
                if active(j, 3):
                    g = j - 3
                    pe.wait_ge(xn2_ready, g + 1)
                    pe.wait_ge(xn1T_ready, KC * min(g + 2, NG) if isinstance(g, int) else KC * (g + 2))
                    for k in range(KC):
                        for i in range(GT):
                            t = turn(bank[k][:, i * P:(i + 1) * P], xn2[:, i, k * P:(k + 1) * P])
                        t.then_inc(xn2_turned, 1)
                if active(j, 2):
                    g = j - 2
                    pe.wait_ge(prbT_ready, g + 1)
                    wait_count(pe, x1_ready, g)
                    for i in range(GT):
                        t = pe.matmul(bank[4 + i // 2][:, (i % 2) * C:(i % 2 + 1) * C], prbT[:, i * P:(i + 1) * P],
                                      v_sb[:, g // GB, :], start=True, stop=True)
                    t.then_inc(attended, 1)
                if active(j, 1):
                    g = j - 1
                    pe.wait_ge(xn1_ready, g + 1)
                    wait_count(pe, xn1T_ready, KC * g)
                    wait_count(pe, xn2T_ready, KC * (g - 1))
                    for k in range(KC):
                        for i in range(GT):
                            t = turn(bank[k][:, i * P:(i + 1) * P], xn1[:, i, k * P:(k + 1) * P])
                        t.then_inc(xn1_turned, 1)
                if active(j, 3):
                    g = j - 3
                    pe.wait_ge(xn2T_ready, KC * (g + 1))
                    for i in range(GT):
                        for k in range(KC):
                            t = pe.matmul(bank[6][:, bass.ds((g * GT + i) * E, E)], xn2T[:, k, i * P:(i + 1) * P],
                                          gate_sb[:, k, :], start=(k == 0), stop=(k == KC - 1))
                    t.then_inc(gated, 1)
                if active(j, 1):
                    g = j - 1
                    pe.wait_ge(xn1T_ready, KC * (g + 1))
                    wait_count(pe, exp_done, g)
                    for i in range(GT):
                        o = bank[2][:, i * S:(i + 1) * S]
                        for k in range(KC):
                            pe.matmul(o, xn1T[:, k, i * P:(i + 1) * P], qk[:, k, bass.ts(g // GB, S)],
                                      start=(k == 0), stop=False)
                        t = pe.matmul(o, ones_row[:], qk_bias[:, bass.ts(g // GB, S)], start=False, stop=True)
                    t.then_inc(scored, 1)

            run_steps(pe, step)

            pe.wait_ge(consts, 12)
            counts = bank[0][:, 0:B * KT * E].rearrange("p (b n) -> p b n", b=B)
            with pe.Fori(0, ROUNDS) as r:
                pe.wait_ge(over_ready, r + 1)
                for c in range(TC):
                    t = pe.matmul(counts, onesb[:], over[:, :, c, :], start=(c == 0), stop=(c == TC - 1))
                t.then_inc(counted, 1)
            pe.wait_ge(masks, 2)

            def shape4(ap):
                return ap.rearrange("p (b c e) -> p b c e", b=B, c=TC)

            def over_all(ap):
                return ap.unsqueeze(2).to_broadcast([P, B, TC, E])

            for dst, m in ((bank[1], above), (bank[2], tied)):
                o = shape4(dst[:, 0:NC * E])
                for c in range(TC):
                    pe.matmul(o, before[:], over_all(m[:, :, c, :]), start=(c == 0), stop=False,
                              skip_group_check=True)
                if m is tied:
                    for c in range(TC):
                        pe.matmul(o, onesb[:], over_all(above[:, :, c, :]), start=False, stop=False,
                                  skip_group_check=True)
                for c in range(TC):
                    t = pe.matmul(o[:, :, c:TC, :], identb[:],
                                  m[:, :, c, :].unsqueeze(2).to_broadcast([P, B, TC - c, E]),
                                  start=False, stop=(c == TC - 1), skip_group_check=True)
                t.then_inc(ranked, 1)

            def list_batch(b, n):
                pe.wait_ge(onehot_ready, n)
                for c in range(TC):
                    t = pe.matmul(bank[3][:, b * LB:(b + 1) * LB], onehot[:, b * TC + c, :], val_e[:, b * TC + c, :],
                                  start=(c == 0), stop=(c == TC - 1))
                t.then_inc(listed, 1)

            def turn_rows(g, k, n, first=False):
                if not first:
                    pe.wait_ge(x_split, n)
                for i in range(NL):
                    t = turn(bank[2][:, i * P:(i + 1) * P], xg[g][:, i, k * P:(k + 1) * P])
                t.then_inc(xg_turned, 1)

            def ff1(s, n, e):
                g, j = s // HC, s % HC
                if j == 0:
                    pe.wait_ge(x_split, 2 * NU * e + 2 * (g + 1))
                if g == 0:
                    pe.wait_ge(w1_split, HC * e + j + 1)
                if not (isinstance(n, int) and n < 2):
                    pe.wait_ge(gelu_done, n - 1)
                m = 0
                for w, xx in ((w1hi, xhi), (w1hi, xlo), (w1lo, xhi)):
                    for k in range(KC):
                        t = pe.matmul(bank[s % 2][:], w[:, j, k, :], xx[g][:, k, :], start=(m == 0), stop=(m == 5))
                        m += 1
                t.then_inc(ff1_done, 1)

            def ff2(s, n, e):
                g, j = s // HC, s % HC
                if g == 0:
                    pe.wait_ge(w2_split, HC * e + j + 1)
                pe.wait_ge(h_split, n + 1)
                for i in range(NL):
                    o = bank[4 + 2 * g + i // 2][:, (i % 2) * C:(i % 2 + 1) * C]
                    for m, (hh, w) in enumerate(((hhi, w2hi), (hhi, w2lo), (hlo, w2hi))):
                        t = pe.matmul(o, hh[s % 4][:, i * P:(i + 1) * P], w[:, j, :],
                                      start=(j == 0 and m == 0 and i % 2 == 0), stop=(j == HC - 1 and m == 2),
                                      skip_group_check=True)
                t.then_inc(ff2_done, 1)

            for b in range(B):
                list_batch(b, b + 1)
            pe.wait_ge(gathered[0], 16 * 2 * NL)
            pe.wait_ge(ranked, 2)
            pe.wait_ge(placed, 3)
            for k in range(KC):
                turn_rows(0, k, k, first=(k == 0))
            ff1(0, 0, 0)
            ff1(1, 1, 0)

            def expert(e, last):
                for s in range(ST):
                    if s + 2 < ST:
                        ff1(s + 2, ST * e + s + 2, e)
                    elif not last:
                        ff1(s + 2 - ST, ST * e + s + 2, e + 1)
                    if s == 1:
                        pe.wait_ge(gathered[1], 16 * 2 * NL * (e + 1))
                    if s in (1, 2):
                        turn_rows(1, s - 1, 2 * NU * e + 1 + s)
                    if s == 10 and not last:
                        pe.wait_ge(gathered[0], 16 * 2 * NL * (e + 2))
                    if s in (10, 11) and not last:
                        turn_rows(0, s - 10, 2 * NU * (e + 1) + s - 10)
                    if 1 <= s <= B and not last:
                        list_batch(s - 1, B * (e + 1) + s)
                    ff2(s, ST * e + s, e)

            run_experts(pe, expert)

        @block.vector
        def _(dve):
            def stats(src, st, mv, ve, done, var, g):
                keep_wait(dve, dve_passed)
                for i in range(GT):
                    dve.bn_stats(st[:, i, :], src[:, i, :]).then_inc(done, 1)
                for i in range(GT):
                    dve.wait_ge(done, 2 * GT * g + i + 1)
                    keep_wait(dve, dve_passed)
                    dve.bn_aggr(mv[:, i, :], st[:, i, :]).then_inc(done, 1)
                dve.wait_ge(done, 2 * GT * (g + 1))
                dve.tensor_scalar(ve[:], mv[:, :, 1], EPS, None, ALU.add).then_inc(var, 1)

            def normed(dst, src, mv, rs, ready):
                for i in range(GT):
                    t = dve.tensor_scalar(dst[:, i, :], src[:, i, :], mv[:, i, 0:1], rs[:, i:i + 1],
                                          ALU.subtract, ALU.mult)
                t.then_inc(ready, 1)

            dve.wait_ge(x_first, 16)

            def step(j):
                if isinstance(j, int) and j == GB:
                    dve.wait_ge(x_rest, 16 * (B - 1))
                if active(j, 3):
                    g = j - 3
                    dve.wait_ge(rstd2, g + 1)
                    wait_count(dve, xn2_turned, KC * g)
                    wait_count(dve, xn_stored, 16 * g)
                    normed(xn2, xcols(g), mv2, rs2, xn2_ready)
                if active(j, 1):
                    g = j - 1
                    dve.wait_ge(rstd1, g + 1)
                    wait_count(dve, xn1_turned, KC * g)
                    normed(xn1, xcols(g), mv1, rs1, xn1_ready)
                if active(j, 0):
                    stats(xcols(j), st1, mv1, ve1, stats1, var1, j)
                if active(j, 2):
                    g = j - 2
                    dve.wait_ge(exp_done, g + 1)
                    dve.reciprocal(rinv[:], psums[:]).then_inc(rinv_ready, 1)
                    dve.wait_ge(rinv_ready, g + 1)
                    dve.wait_ge(attended, g + 1)
                    xc = xcols(g)
                    for i in range(GT):
                        t = dve.scalar_tensor_tensor(out=xc[:, i, :], in0=bank[4 + i // 2][:, (i % 2) * C:(i % 2 + 1) * C],
                                                     scalar=rinv[:, i:i + 1], in1=xc[:, i, :], op0=ALU.mult, op1=ALU.add)
                    t.then_inc(x1_ready, 1)
                    dve.wait_ge(x1_ready, g + 1)
                    stats(xc, st2, mv2, ve2, stats2, var2, g)
                if active(j, 1):
                    g = j - 1
                    dve.wait_ge(scored, g + 1)
                    dve.tensor_reduce(nmax[:], bank[2][:, 0:GT * S].rearrange("p (i s) -> p i s", i=GT), AX.X, ALU.max,
                                      negate=True).then_inc(max_ready, 1)

            run_steps(dve, step)

            logits = bank[6][:, 0:NC * E].rearrange("p (n e) -> p n e", e=E)
            pr = prob[:].rearrange("p b c e -> p (b c) e")
            dve.wait_ge(gated, NG)
            dve.tensor_reduce(gmax[:], logits, AX.X, ALU.max).then_inc(soft, 1)
            dve.wait_ge(soft, 1)
            dve.tensor_tensor(pr, logits, gmax[:].unsqueeze(2).to_broadcast([P, NC, E]), ALU.subtract).then_inc(soft, 1)
            dve.wait_ge(gexp, 1)
            dve.tensor_reduce(gsum[:], pr, AX.X, ALU.add).then_inc(soft, 1)
            dve.wait_ge(soft, 3)
            dve.reciprocal(gmax[:], gsum[:]).then_inc(soft, 1)
            dve.wait_ge(soft, 4)
            dve.tensor_tensor(pr, pr, gmax[:].unsqueeze(2).to_broadcast([P, NC, E]), ALU.mult).then_inc(soft, 1)

            dve.wait_ge(consts, 12)
            dve.tensor_scalar(cand_off[:], cand_off[:], BITS - RB, None, ALU.logical_shift_left).then_inc(step_ready, 1)
            dve.tensor_scalar(bit_step[:], bit_step[:], 1.0, None, ALU.mult).then_inc(step_ready, 1)
            dve.tensor_copy(gain[:], floor_[:]).then_inc(floor_ready, 1)
            dve.wait_ge(soft, 5)
            with dve.Fori(0, ROUNDS) as r:
                dve.wait_ge(floor_ready, r + 1)
                dve.wait_ge(step_ready, 2 * r + 2)
                for b in range(B):
                    t = dve.tensor_tensor(cand[:, b], floor_[:, b].unsqueeze(1).to_broadcast([P, KT, E]), cand_off[:, b],
                                          ALU.bitwise_or)
                t.then_inc(cand_ready, 1)
                dve.wait_ge(cand_ready, r + 1)
                for b in range(B):
                    t = dve.tensor_tensor(
                        over[:, b].rearrange("p c (k e) -> p c k e", k=KT),
                        prob[:, b].unsqueeze(2).to_broadcast([P, TC, KT, E]),
                        cand[:, b].bitcast(F32).unsqueeze(1).to_broadcast([P, TC, KT, E]), ALU.is_ge)
                t.then_inc(over_ready, 1)
                dve.tensor_scalar(cand_off[:], cand_off[:], RB, None, ALU.logical_shift_right).then_inc(step_ready, 1)
                dve.wait_ge(counted, r + 1)
                dve.tensor_scalar(enough[:].rearrange("p b k e -> p (b k e)"), bank[0][:, 0:B * KT * E], float(CAP),
                                  bit_step[:], ALU.is_ge, ALU.mult).then_inc(enough_ready, 1)
                dve.tensor_scalar(bit_step[:], bit_step[:], 2.0 ** -RB, None, ALU.mult).then_inc(step_ready, 1)
                dve.wait_ge(enough_ready, r + 1)
                with nc.allow_low_precision(reason="at most three equal powers of two: exact"):
                    dve.tensor_reduce(gain[:], enough[:].rearrange("p b k e -> p b e k"), AX.X,
                                      ALU.add).then_inc(gain_ready, 1)
                dve.wait_ge(gain_ready, r + 1)
                dve.tensor_tensor(floor_[:], floor_[:], gain[:], ALU.bitwise_or).then_inc(floor_ready, 1)

            dve.wait_ge(floor_ready, ROUNDS + 1)
            for b in range(B):
                f = floor_[:, b].bitcast(F32).unsqueeze(1).to_broadcast([P, TC, E])
                t = dve.tensor_tensor(above[:, b], prob[:, b], f, ALU.is_gt)
            t.then_inc(masks, 1)
            for b in range(B):
                f = floor_[:, b].bitcast(F32).unsqueeze(1).to_broadcast([P, TC, E])
                t = dve.tensor_tensor(tied[:, b], prob[:, b], f, ALU.is_equal)
            t.then_inc(masks, 1)

            def flat(ap):
                return ap.rearrange("p b c e -> p (b c e)")

            dve.wait_ge(masks, 2)
            dve.wait_ge(ranked, 1)
            dve.tensor_tensor(flat(pos_a[:]), bank[1][:, 0:NC * E], flat(above[:]), ALU.mult).then_inc(placed, 1)
            dve.wait_ge(ranked, 2)
            dve.tensor_tensor(flat(pos_t[:]), bank[2][:, 0:NC * E], flat(tied[:]), ALU.mult).then_inc(placed, 1)
            dve.wait_ge(placed, 2)
            dve.tensor_tensor(pos_a[:], pos_a[:], pos_t[:], ALU.add).then_inc(placed, 1)
            dve.wait_ge(placed, 3)
            dve.tensor_scalar(second[:], pos_a[:], P + 0.5, None, ALU.is_gt).then_inc(placed, 1)
            dve.wait_ge(placed, 4)
            sl = slot_of[:].rearrange("p n e -> p (n e)")
            dve.scalar_tensor_tensor(out=sl, in0=flat(second[:]), scalar=-float(P), in1=flat(pos_a[:]),
                                     op0=ALU.mult, op1=ALU.add).then_inc(placed, 1)
            dve.tensor_tensor(pos_t[:], second[:], tok_no[:], ALU.mult).then_inc(placed, 1)
            dve.wait_ge(placed, 6)
            tv = tok_val[:].rearrange("p n e l -> p (n e) l")
            dve.tensor_copy(tv[:, :, 1], flat(pos_t[:])).then_inc(placed, 1)
            dve.tensor_tensor(tv[:, :, 0], flat(tok_no[:]), flat(pos_t[:]), ALU.subtract).then_inc(placed, 1)
            dve.wait_ge(placed, 8)

            def columns(e, n):
                dve.tensor_copy(slot_e[:].unsqueeze(2), slot_of[:, :, bass.ds(e, 1)]).then_inc(col_ready, 1)
                dve.tensor_copy(val_e[:].unsqueeze(2), tok_val[:, :, bass.ds(e, 1), :]).then_inc(col_ready, 1)
                dve.wait_ge(col_ready, n)

            def one_hot(b):
                for c in range(TC):
                    t = dve.tensor_scalar(onehot[:, b * TC + c, :], slot_no[:], slot_e[:, b * TC + c:b * TC + c + 1],
                                          None, ALU.is_equal)
                t.then_inc(onehot_ready, 1)

            def index_list(n):
                dve.wait_ge(listed, B * n)
                dve.tensor_tensor(gidx[:], bank[3][:, 0:B * LB], row0[:], ALU.add).then_inc(gidx_ready, 1)

            def x_rest_part(g, k, n):
                dve.wait_ge(x_hi, n)
                dve.tensor_tensor(xlo[g][:, k], bank[2][:], xhi[g][:, k].bitcast(F32), ALU.subtract).then_inc(x_split, 1)

            def prob_column(g, e):
                dve.tensor_copy(pcol[g][:].unsqueeze(2), pg[g][:, :, bass.ds(e, 1)]).then_inc(pcol_ready, 1)

            def split_h(s, n):
                dve.wait_ge(gelu_done, n + 1)
                dve.tensor_copy(hhi[s % 4][:], hraw[s % 2][:]).then_inc(h_hi, 1)
                dve.wait_ge(h_hi, n + 1)
                dve.tensor_tensor(hlo[s % 4][:], hraw[s % 2][:], hhi[s % 4][:].bitcast(F32),
                                  ALU.subtract).then_inc(h_split, 1)

            dve.wait_ge(first_split, 2 * HC - 1)
            dve.sem_inc(w1_split, HC)
            dve.sem_inc(w2_split, HC - 1)

            columns(0, 2)
            for b in range(B):
                one_hot(b)
            index_list(1)
            for k in range(KC):
                x_rest_part(0, k, k + 1)
            dve.wait_ge(gathered[0], 16 * 2 * NL)
            prob_column(0, 0)
            split_h(0, 0)
            split_h(1, 1)

            def expert(e, last):
                for s in range(ST):
                    if s == 0:
                        dve.wait_ge(w2_hi, HC * (e + 1))
                        dve.tensor_tensor(w2lo[:, HC - 1], w2raw[:, HC - 1], w2hi[:, HC - 1].bitcast(F32),
                                          ALU.subtract).then_inc(w2_split, 1)
                        if not last:
                            columns(e + 1, 2 * (e + 2))
                    if s in (1, 2):
                        x_rest_part(1, s - 1, 2 * NU * e + 2 + s)
                    if s == 2:
                        dve.wait_ge(gathered[1], 16 * 2 * NL * (e + 1))
                        prob_column(1, e)
                    if s < B and not last:
                        one_hot(s)
                    if s == 4:
                        dve.wait_ge(settled, e + 1)
                        dve.tensor_copy(sidx[:], gidx[:]).then_inc(sidx_ready, 1)
                    if s == 5 and not last:
                        dve.wait_ge(sidx_ready, e + 1)
                        index_list(e + 2)
                    if s in (10, 11) and not last:
                        x_rest_part(0, s - 10, 2 * NU * (e + 1) + s - 9)
                    if s == 11 and not last:
                        dve.wait_ge(gathered[0], 16 * 2 * NL * (e + 2))
                        dve.wait_ge(y_ready, 2 * e + 1)
                        prob_column(0, e + 1)
                    if HC - 1 <= s < 2 * HC - 1 and not last:
                        j = s - (HC - 1)
                        dve.wait_ge(w1_hi, HC * (e + 1) + j + 1)
                        dve.tensor_tensor(w1lo[:, j], w1raw[:, :, bass.ts(j, P)], w1hi[:, j].bitcast(F32),
                                          ALU.subtract).then_inc(w1_split, 1)
                    if s > HC and not last:
                        j = s - HC - 1
                        dve.wait_ge(w2_hi, HC * (e + 1) + j + 1)
                        dve.tensor_tensor(w2lo[:, j], w2raw[:, j], w2hi[:, j].bitcast(F32),
                                          ALU.subtract).then_inc(w2_split, 1)
                    if s + 2 < ST or not last:
                        split_h(s + 2, ST * e + s + 2)

            run_experts(dve, expert)


_INS = ['x', 'ctx_1024', 'L0_xattn_Wq', 'L0_xattn_bq', 'L0_xattn_Wk', 'L0_xattn_bk', 'L0_xattn_Wv', 'L0_xattn_bv',
        'L0_ffn_gate_w', 'L0_ffn_w1', 'L0_ffn_w2']


def kernel(**inputs):
    import numpy as _np
    import concourse.bacc as _bacc
    from concourse import mybir as _mybir
    from concourse.bass_utils import run_bass_kernel_spmd as _run

    nc = _bacc.Bacc("TRN2", target_bir_lowering=False, num_devices=1)
    arrays, args = {}, []
    for name in _INS:
        a = _np.ascontiguousarray(inputs[name])
        arrays[f"in_{name}_dram"] = a
        args.append(nc.dram_tensor(f"in_{name}_dram", a.shape, _mybir.dt.from_np(a.dtype), kind="ExternalInput").ap())
    args.append(nc.dram_tensor("out_0_dram", inputs['x'].shape, _mybir.dt.float32, kind="ExternalOutput").ap())
    build(nc, *args)
    r = _run(nc, [arrays], core_ids=[0])
    return r.results[0]["out_0_dram"]
```

```python
from contextlib import ExitStack

import concourse.bass as bass
from concourse import mybir

F32 = mybir.dt.float32
F32R = mybir.dt.float32r
BF16 = mybir.dt.bfloat16
F16 = mybir.dt.float16
I32 = mybir.dt.int32
ALU = mybir.AluOpType
ACT = mybir.ActivationFunctionType
AX = mybir.AxisListType

P = 128
EPS = 1e-5


def wait_count(eng, sem, n):
    if isinstance(n, int) and n <= 0:
        return
    eng.wait_ge(sem, n)


def build(nc, x, ctx_in, Wq, bq, Wk, bk, Wv, bv, gate_w, w1, w2, out):
    B, T, C = x.shape
    S = ctx_in.shape[1]
    E, _, H = w1.shape
    CAP = 2 * T // E
    TC = T // P
    NC = B * TC
    KC = C // P
    HC = H // P
    GT = 4
    NG = NC // GT
    GB = TC // GT
    LB = CAP // P
    UB = 2
    NU = B // UB
    NL = UB * LB
    UT = NL * P
    ST = NU * HC
    BITS, RB = 30, 2
    KT = 2 ** RB - 1
    ROUNDS = BITS // RB
    HB = B // 2
    EX = E + 1
    SX = S + EX
    CX = C + EX
    assert KC == 2 and UT == 512 and B * S == 2 * P and NC * E == 256

    xn_dram = nc.dram_tensor("xn_rows", (B * T, C), F32, kind="Internal").ap()
    pr_dram = nc.dram_tensor("prob_rows", (B * T, E), F32, kind="Internal").ap()

    x_v = x.rearrange("b (p c) d -> b p c d", c=TC)
    out_v = out.rearrange("b (p c) d -> p b c d", c=TC)
    xn_v = xn_dram.rearrange("(b p c) d -> p b c d", b=B, c=TC)
    pr_v = pr_dram.rearrange("(b p c) e -> p b (c e)", b=B, c=TC)
    out_rows = out.rearrange("b t d -> (b t) d")

    with ExitStack() as stack:
        def sb(name, shape, dt):
            return stack.enter_context(nc.sbuf_tensor(name, shape, dt))

        def sem(name):
            return stack.enter_context(nc.semaphore(name))

        bank = [stack.enter_context(nc.psum_tensor(f"bank{i}", [P, 512], F32)) for i in range(4)]
        wide = stack.enter_context(nc.psum_tensor("wide", [P, 4, 512], F32))
        bank += [wide[:, i] for i in range(4)]

        identf = sb("identf", [P, P], F32)
        identb = sb("identb", [P, P], BF16)
        onesb = sb("onesb", [P, P], BF16)
        before = sb("before", [P, P], BF16)
        ones_row = sb("ones_row", [1, P], F32)
        slot_no = sb("slot_no", [P, P], F16)
        tok_no = sb("tok_no", [P, B, TC, E], F32)
        row0 = sb("row0", [P, B * LB], F32)
        neghalf = sb("neghalf", [P, NC], F32)
        inv_c = sb("inv_c", [P, P], F32)
        cand_off = sb("cand_off", [P, B, KT, E], I32)
        wk_sb = sb("wk_sb", [P, KC, C], F32)
        wq_sb = sb("wq_sb", [P, KC, C], F32)
        wv_sb = sb("wv_sb", [P, KC, C], F32)
        ctx_sb = sb("ctx_sb", [P, KC, C], F32)
        bk_sb = sb("bk_sb", [P, KC], F32)
        bq_sb = sb("bq_sb", [P, KC], F32)
        bv_ext = sb("bv_ext", [1, CX], F32)
        bv_col = sb("bv_col", [P, KC], F32)
        gate_sb = sb("gate_sb", [P, KC, E], F32)
        ctxT = sb("ctxT", [P, KC, B * S], F32)
        wkT = sb("wkT", [P, KC, C], F32)
        wvT = sb("wvT", [P, KC, CX], F32)
        kT = sb("kT", [P, KC, B * S], F32)
        qk = sb("qk", [P, KC, B, SX], F32)
        qk_bias = sb("qk_bias", [P, B, S], F32)
        v_sb = sb("v_sb", [S, B, CX], F32)
        x_all = sb("x_all", [P, B, TC, C], F32)
        st1 = sb("st1", [P, GT, 6], F32)
        mv1 = sb("mv1", [P, GT, 2], F32)
        ve1 = sb("ve1", [P, GT], F32)
        rs1 = sb("rs1", [P, GT], F32)
        nm1 = sb("nm1", [P, NC], F32)
        xc = sb("xc", [P, GT, C], F32)
        xcT = sb("xcT", [P, KC, GT * P], F32)
        score = sb("score", [P, GT, S], F32)
        nmax = sb("nmax", [P, GT], F32)
        prb = sb("prb", [P, GT, S], F32)
        psums = sb("psums", [P, GT], F32)
        prbT = sb("prbT", [S, GT * P], F32)
        rinv = sb("rinv", [P, GT], F32)
        extra = sb("extra", [P, NC, EX], F32)
        extra_v = sb("extra_v", [P, GT, EX], F32)
        nm2 = sb("nm2", [P, NC], F32)
        sq = sb("sq", [P, GT, C], F32)
        ss2 = sb("ss2", [P, NC], F32)
        ve2 = sb("ve2", [P, NC], F32)
        rs2 = sb("rs2", [P, NC], F32)
        nb2 = sb("nb2", [P, NC], F32)
        gmax = sb("gmax", [P, NC], F32)
        gsum = sb("gsum", [P, NC], F32)
        prob = sb("prob", [P, B, TC, E], F32)
        floor_ = sb("floor", [P, B, E], F32)
        cand = sb("cand", [P, B, KT, E], I32)
        over = sb("over", [P, B, TC, KT * E], BF16)
        reached = sb("reached", [P, B, KT + 1, E], F32)
        above = sb("above", [P, B, TC, E], BF16)
        tied = sb("tied", [P, B, TC, E], BF16)
        pos_a = sb("pos_a", [P, B, TC, E], F32)
        pos_t = sb("pos_t", [P, B, TC, E], F32)
        second = sb("second", [P, B, TC, E], F32)
        slot_of = sb("slot_of", [P, B * TC, E], F32)
        tok_val = sb("tok_val", [P, B * TC, E, LB], F16)
        slot_e = sb("slot_e", [P, B * TC], F32)
        val_e = sb("val_e", [P, B * TC, LB], F16)
        onehot = sb("onehot", [P, B * TC, P], F16)
        gidx = sb("gidx", [P, B * LB], I32)
        sidx = sb("sidx", [P, B * LB], I32)
        w1raw = sb("w1raw", [P, KC, H], F32)
        w2raw = sb("w2raw", [P, HC, C], F32)
        w1hi = sb("w1hi", [P, HC, KC, P], F32R)
        w1lo = sb("w1lo", [P, HC, KC, P], F32R)
        w2hi = sb("w2hi", [P, HC, C], F32R)
        w2lo = sb("w2lo", [P, HC, C], F32R)
        xg = [sb(f"xg{g}", [P, NL, C], F32) for g in range(NU)]
        pg = [sb(f"pg{g}", [P, NL, E], F32) for g in range(NU)]
        pcol = [sb(f"pcol{g}", [P, NL], F32) for g in range(NU)]
        xhi = [sb(f"xhi{g}", [P, KC, UT], F32R) for g in range(NU)]
        xlo = [sb(f"xlo{g}", [P, KC, UT], F32R) for g in range(NU)]
        hraw = [sb(f"hraw{i}", [P, UT], F32) for i in range(2)]
        hhi = [sb(f"hhi{i}", [P, UT], F32R) for i in range(4)]
        hlo = [sb(f"hlo{i}", [P, UT], F32R) for i in range(4)]
        ysb = [sb(f"ysb{g}", [P, NL, C], F32) for g in range(NU)]

        kv_loaded = sem("kv_loaded")
        q_loaded = sem("q_loaded")
        v_loaded = sem("v_loaded")
        x_first = sem("x_first")
        x_second = sem("x_second")
        x_rest = sem("x_rest")
        consts = sem("consts")
        bits_set = sem("bits_set")
        folded = sem("folded")
        ctxT_ready = sem("ctxT_ready")
        wkT_ready = sem("wkT_ready")
        kT0_ready = sem("kT0_ready")
        kT1_ready = sem("kT1_ready")
        gate_ready = sem("gate_ready")
        qk_ready = sem("qk_ready")
        qk_bias_ready = sem("qk_bias_ready")
        wvT_ready = sem("wvT_ready")
        v_ready = sem("v_ready")
        stats1 = sem("stats1")
        mean1 = sem("mean1")
        var1 = sem("var1")
        rstd1 = sem("rstd1")
        xc_ready = sem("xc_ready")
        xc_turned = sem("xc_turned")
        xcT_ready = sem("xcT_ready")
        scored = sem("scored")
        score_ready = sem("score_ready")
        max_ready = sem("max_ready")
        exp_done = sem("exp_done")
        prb_turned = sem("prb_turned")
        prbT_ready = sem("prbT_ready")
        attended = sem("attended")
        rinv_ready = sem("rinv_ready")
        extra_ready = sem("extra_ready")
        x1_ready = sem("x1_ready")
        squared = sem("squared")
        ve2_ready = sem("ve2_ready")
        rstd2 = sem("rstd2")
        nb2_ready = sem("nb2_ready")
        xn2_ready = sem("xn2_ready")
        rows_stored = sem("rows_stored")
        rows_added = sem("rows_added")
        settled = sem("settled")
        xn_stored = sem("xn_stored")
        soft = sem("soft")
        gexp = sem("gexp")
        pr_stored = sem("pr_stored")
        floor_set = sem("floor_set")
        off_ready = [sem(f"off_ready{h}") for h in range(2)]
        cand_ready = [sem(f"cand_ready{h}") for h in range(2)]
        over_ready = [sem(f"over_ready{h}") for h in range(2)]
        counted = [sem(f"counted{h}") for h in range(2)]
        reached_ready = [sem(f"reached_ready{h}") for h in range(2)]
        floor_ready = [sem(f"floor_ready{h}") for h in range(2)]
        masks = sem("masks")
        ranked = sem("ranked")
        placed = sem("placed")
        col_ready = sem("col_ready")
        onehot_ready = sem("onehot_ready")
        listed = sem("listed")
        gidx_ready = sem("gidx_ready")
        sidx_ready = sem("sidx_ready")
        raw_loaded = sem("raw_loaded")
        w1_hi = sem("w1_hi")
        w2_hi = sem("w2_hi")
        first_split = sem("first_split")
        w1_split = sem("w1_split")
        w2_split = sem("w2_split")
        gathered = [sem(f"gathered{g}") for g in range(NU)]
        xg_turned = sem("xg_turned")
        x_hi = sem("x_hi")
        x_split = sem("x_split")
        pcol_ready = sem("pcol_ready")
        ff1_done = sem("ff1_done")
        gelu_done = sem("gelu_done")
        h_hi = sem("h_hi")
        h_split = sem("h_split")
        ff2_done = sem("ff2_done")
        y_ready = sem("y_ready")

        dve_passed = sem("dve_passed")
        pe_passed = sem("pe_passed")
        pool_passed = sem("pool_passed")

        def keep_wait(eng, passed):
            eng.sem_inc(passed, 1)

        LAST = 3

        def active(j, stage):
            return not isinstance(j, int) or 0 <= j - stage < NG

        def run_steps(eng, body, after={}):
            for j in range(LAST + 1):
                body(j)
                if j in after:
                    after[j]()
            with eng.Fori(LAST + 1, NG) as j:
                body(j)
            for j in range(NG, NG + LAST):
                body(j)

        def columns_of(ap, g):
            return ap[:, bass.ts(g, GT)]

        def xcols(g):
            return x_all[:].rearrange("p b c d -> p (b c) d")[:, bass.ts(g, GT), :]

        def run_experts(eng, body):
            with eng.Fori(0, E - 1) as e:
                body(e, False)
            body(E - 1, True)

        block = stack.enter_context(nc.Block())

        @block.sync
        def _(sp):
            x_g = x.rearrange("b (p q c) d -> p b q (c d)", q=GB, c=GT)
            sp.dma_start(wk_sb[:], Wk.rearrange("(k p) d -> p k d", p=P)).then_inc(kv_loaded, 16)
            sp.dma_start(ctx_sb[:], ctx_in.rearrange("b s d -> (b s) d").rearrange("(k p) d -> p k d", p=P)).then_inc(kv_loaded, 16)
            sp.dma_start(bk_sb[:], bk.rearrange("(k p) -> p k", p=P), allow_slow_non_contiguous=True).then_inc(kv_loaded, 16)
            sp.dma_start(xcols(0), x_g[:, 0, 0]).then_inc(x_first, 16)
            sp.dma_start(wq_sb[:], Wq.rearrange("(k p) d -> p k d", p=P)).then_inc(q_loaded, 16)
            sp.dma_start(bq_sb[:], bq.rearrange("(k p) -> p k", p=P), allow_slow_non_contiguous=True).then_inc(q_loaded, 16)
            sp.dma_start(gate_sb[:], gate_w.rearrange("(k p) e -> p k e", p=P)).then_inc(q_loaded, 16)
            sp.dma_start(xcols(1), x_g[:, 0, 1]).then_inc(x_second, 16)
            sp.dma_start(wv_sb[:], Wv.rearrange("(k p) d -> p k d", p=P)).then_inc(v_loaded, 16)
            sp.dma_start(bv_ext[:, 0:C], bv.rearrange("(a d) -> a d", a=1)).then_inc(v_loaded, 16)
            sp.dma_start(bv_col[:], bv.rearrange("(k p) -> p k", p=P), allow_slow_non_contiguous=True).then_inc(v_loaded, 16)
            for b in range(1, B):
                sp.dma_start(x_all[:, b], x_v[b]).then_inc(x_rest, 16)
            sp.dma_start(w1raw[:], w1[0].rearrange("(k p) h -> p k h", p=P)).then_inc(raw_loaded, 16)
            sp.dma_start(w2raw[:], w2[0].rearrange("(k p) d -> p k d", p=P)).then_inc(raw_loaded, 16)

            out_g = out.rearrange("b (p q c) d -> p b q (c d)", q=GB, c=GT)

            def step(j):
                if active(j, 3):
                    g = j - 3
                    sp.wait_ge(x1_ready, GT * (g + 1))
                    sp.dma_start(out_g[:, g // GB, g % GB], xcols(g)).then_inc(rows_stored, 16)

            run_steps(sp, step)
            for b in range(B):
                sp.wait_ge(xn2_ready, GB * (b + 1))
                sp.dma_start(xn_v[:, b], x_all[:, b]).then_inc(xn_stored, 16)
            sp.wait_ge(soft, 6)
            sp.dma_start(pr_v, prob[:].rearrange("p b c e -> p b (c e)")).then_inc(pr_stored, 16)

            def load_next(e, last):
                if not last:
                    sp.wait_ge(w2_split, HC * (e + 1))
                    sp.dma_start(w1raw[:], w1_v[:, e + 1]).then_inc(raw_loaded, 16)
                    sp.dma_start(w2raw[:], w2_v[:, e + 1]).then_inc(raw_loaded, 16)

            w1_v = w1.rearrange("e (k p) h -> p e k h", p=P)
            w2_v = w2.rearrange("e (k p) d -> p e k d", p=P)
            run_experts(sp, load_next)

        @block.gpsimd
        def _(pool):
            pool.memset(identf[:], 0.0).then_inc(bits_set, 1)
            pool.memset(identb[:], 0.0).then_inc(bits_set, 1)
            pool.memset(before[:], 1.0).then_inc(bits_set, 1)
            pool.memset(ones_row[:], 1.0).then_inc(consts, 1)
            pool.memset(inv_c[:], 1.0 / C).then_inc(consts, 1)
            pool.memset(qk[:, :, :, SX - 1:SX], 1.0 / C).then_inc(consts, 1)
            pool.memset(neghalf[:], -0.5).then_inc(consts, 1)
            pool.wait_ge(bits_set, 3)
            for m in (identf, identb):
                pool.affine_select(out=m[:], in_=m[:], compare_op=ALU.not_equal, fill=1.0, base=0,
                                   pattern=[[-1, P]], channel_multiplier=1).then_inc(consts, 1)
            pool.affine_select(out=before[:], in_=before[:], compare_op=ALU.is_gt, fill=0.0, base=0,
                               pattern=[[1, P]], channel_multiplier=-1).then_inc(consts, 1)
            pool.memset(onesb[:], 1.0).then_inc(consts, 1)
            pool.memset(floor_[:], 0.0).then_inc(consts, 1)
            pool.iota(cand_off[:], [[0, B], [1, KT], [0, E]], base=1, channel_multiplier=0).then_inc(consts, 1)
            pool.iota(slot_no[:], [[1, P]], base=1, channel_multiplier=0,
                      allow_small_or_imprecise_dtypes=True).then_inc(consts, 1)
            pool.iota(tok_no[:], [[0, B], [1, TC], [0, E]], base=0, channel_multiplier=TC,
                      allow_small_or_imprecise_dtypes=True).then_inc(consts, 1)
            pool.iota(row0[:], [[T, B], [0, LB]], base=0, channel_multiplier=0,
                      allow_small_or_imprecise_dtypes=True).then_inc(consts, 1)

            pool.wait_ge(consts, 4)

            def step(j):
                if active(j, 0):
                    g = j
                    pool.wait_ge(var1, g + 1)
                    wait_count(pool, score_ready, g)
                    pool.tensor_tensor(rs1[:], ve1[:], neghalf[:, 0:GT], ALU.pow).then_inc(rstd1, 1)

            run_steps(pool, step)
            pool.wait_ge(ve2_ready, 1)
            pool.tensor_tensor(rs2[:], ve2[:], neghalf[:], ALU.pow).then_inc(rstd2, 1)

            for j in range(HC):
                pool.wait_ge(w1_hi, j + 1)
                pool.tensor_tensor(w1lo[:, j], w1raw[:, :, bass.ts(j, P)], w1hi[:, j].bitcast(F32),
                                   ALU.subtract).then_inc(first_split, 1)
            for j in range(HC - 1):
                pool.wait_ge(w2_hi, j + 1)
                pool.tensor_tensor(w2lo[:, j], w2raw[:, j], w2hi[:, j].bitcast(F32),
                                   ALU.subtract).then_inc(first_split, 1)

            def gather(g, e):
                keep_wait(pool, pool_passed)
                for i in range(NL):
                    at = bass.IndirectOffsetOnAxis(ap=gidx[:, g * NL + i:g * NL + i + 1], axis=0)
                    pool.indirect_dma_start(out=xg[g][:, i, :], out_offset=None, in_=xn_dram,
                                            in_offset=at).then_inc(gathered[g], 16)
                for i in range(NL):
                    at = bass.IndirectOffsetOnAxis(ap=gidx[:, g * NL + i:g * NL + i + 1], axis=0)
                    pool.indirect_dma_start(out=pg[g][:, i, :], out_offset=None, in_=pr_dram,
                                            in_offset=at).then_inc(gathered[g], 16)

            def scatter(g):
                keep_wait(pool, pool_passed)
                for i in range(NL):
                    at = bass.IndirectOffsetOnAxis(ap=sidx[:, g * NL + i:g * NL + i + 1], axis=0)
                    pool.indirect_dma_start(out=out_rows, out_offset=at, in_=ysb[g][:, i, :], in_offset=None,
                                            compute_op=ALU.add).then_inc(rows_added, 16)

            pool.wait_ge(xn_stored, 16 * B)
            pool.wait_ge(pr_stored, 16)
            pool.wait_ge(gidx_ready, 1)
            gather(0, 0)
            gather(1, 0)

            def expert(e, last):
                if not last:
                    pool.wait_ge(gidx_ready, e + 2)
                    pool.wait_ge(xg_turned, 2 * NU * e + 4)
                    gather(0, e + 1)
                pool.wait_ge(sidx_ready, e + 1)
                pool.wait_ge(y_ready, 2 * e + 1)
                scatter(0)
                if not last:
                    pool.wait_ge(pcol_ready, 2 * e + 2)
                    gather(1, e + 1)
                pool.wait_ge(y_ready, 2 * e + 2)
                scatter(1)
                pool.wait_ge(rows_added, 16 * NU * NL * (e + 1))
                pool.sem_inc(settled, 1)

            pool.wait_ge(rows_stored, 16 * NG)
            pool.sem_inc(settled, 1)
            run_experts(pool, expert)

        @block.scalar
        def _(act):
            act.wait_ge(folded, 1)
            act.activation(ctxT[:].rearrange("p k s -> p (k s)"), bank[0][:], ACT.Copy).then_inc(ctxT_ready, 1)

            def setup():
                act.wait_ge(kv_loaded, 48)
                act.wait_ge(folded, 3)
                act.activation(kT[:, 0], bank[3][:, 0:256], ACT.Identity, bias=bk_sb[:, 0:1]).then_inc(kT0_ready, 1)
                act.wait_ge(folded, 5)
                act.activation(wvT[:, :, 0:C], bank[2][:].rearrange("p (k s) -> p k s", k=KC), ACT.Copy).then_inc(wvT_ready, 1)
                act.wait_ge(folded, 6)
                act.activation(qk[:, :, :, 0:S], wide[:, 0].rearrange("p (k b s) -> p k b s", k=KC, b=B),
                               ACT.Copy).then_inc(qk_ready, 1)
                act.wait_ge(folded, 8)
                act.activation(wvT[:, :, C:CX], wide[:, 2, 16:16 + KC * EX].rearrange("p (k s) -> p k s", k=KC),
                               ACT.Copy).then_inc(wvT_ready, 1)
                act.activation(bv_ext[:, C:CX], wide[0:1, 2, 64:64 + EX], ACT.Copy).then_inc(wvT_ready, 1)

            def values():
                act.wait_ge(folded, 9)
                act.activation(v_sb[:], wide[0:S, :, 0:CX], ACT.Copy).then_inc(v_ready, 1)

            def step(j):
                if active(j, 1):
                    g = j - 1
                    for k in range(KC):
                        act.wait_ge(xc_turned, KC * g + k + 1)
                        act.activation(xcT[:, k], bank[k][:], ACT.Copy).then_inc(xcT_ready, 1)
                if active(j, 2):
                    g = j - 2
                    act.wait_ge(prb_turned, g + 1)
                    act.activation(prbT[:], bank[3][0:S, :], ACT.Copy).then_inc(prbT_ready, 1)
                if active(j, 0):
                    g = j
                    act.wait_ge(mean1, g + 1)
                    m = columns_of(nm1, g)
                    for i in range(GT):
                        a = act.activation(xc[:, i, :], xcols(g)[:, i, :], ACT.Identity, bias=m[:, i:i + 1])
                    a.then_inc(xc_ready, 1)
                if active(j, 3):
                    g = j - 3
                    wait_count(act, squared, GT * g)
                    act.wait_ge(extra_ready, 3 * g + 3)
                    m, ss = columns_of(nm2, g), columns_of(ss2, g)
                    for i in range(GT):
                        act.wait_ge(x1_ready, GT * g + i + 1)
                        act.activation(sq[:, i, :], xcols(g)[:, i, :], ACT.Square, bias=m[:, i:i + 1],
                                       accum_out=ss[:, i:i + 1]).then_inc(squared, 1)
                if active(j, 1):
                    g = j - 1
                    act.wait_ge(max_ready, g + 1)
                    for i in range(GT):
                        a = act.activation(prb[:, i, :], score[:, i, :], ACT.Exp, bias=nmax[:, i:i + 1],
                                           accum_out=psums[:, i:i + 1])
                    a.then_inc(exp_done, 1)

            run_steps(act, step, {0: setup, 1: values})

            act.wait_ge(soft, 3)
            pr = prob[:].rearrange("p b c e -> p (b c e)")
            act.activation(pr, pr, ACT.Exp).then_inc(gexp, 1)

            act.wait_ge(rows_stored, 16 * NG)
            act.wait_ge(nb2_ready, 1)
            with act.Fori(0, NG) as g:
                m, rs = columns_of(nb2, g), columns_of(rs2, g)
                for i in range(GT):
                    a = act.activation(xcols(g)[:, i, :], xcols(g)[:, i, :], ACT.Identity, bias=m[:, i:i + 1],
                                       scale=rs[:, i:i + 1])
                a.then_inc(xn2_ready, 1)

            def w1_part(j, n):
                act.activation(w1hi[:, j], w1raw[:, :, bass.ts(j, P)], ACT.Copy).then_inc(w1_hi, 1)

            def w2_part(j, n):
                act.activation(w2hi[:, j], w2raw[:, j], ACT.Copy).then_inc(w2_hi, 1)

            act.wait_ge(raw_loaded, 32)
            for j in range(HC):
                w1_part(j, 0)
            for j in range(HC - 1):
                w2_part(j, 0)

            def x_part(g, k, n):
                act.wait_ge(xg_turned, n)
                act.activation(xhi[g][:, k], bank[2][:], ACT.Copy).then_inc(x_hi, 1)

            def gelu(s, n):
                act.wait_ge(ff1_done, n + 1)
                if not (isinstance(n, int) and n < 2):
                    act.wait_ge(h_split, n - 1)
                act.activation(hraw[s % 2][:], bank[s % 2][:], ACT.Gelu).then_inc(gelu_done, 1)

            def y_rows(g, e):
                act.wait_ge(ff2_done, ST * e + HC * (g + 1))
                act.wait_ge(pcol_ready, 2 * e + g + 1)
                if g == 0:
                    act.wait_ge(settled, e + 1)

                for i in range(NL):
                    a = act.activation(ysb[g][:, i, :], bank[4 + 2 * g + i // 2][:, (i % 2) * C:(i % 2 + 1) * C],
                                       ACT.Copy, scale=pcol[g][:, i:i + 1])
                a.then_inc(y_ready, 1)

            for k in range(KC):
                x_part(0, k, k + 1)
            gelu(0, 0)
            gelu(1, 1)

            def expert(e, last):
                for s in range(ST):
                    if s in (1, 2):
                        x_part(1, s - 1, 2 * NU * e + 2 + s)
                    if s in (10, 11) and not last:
                        x_part(0, s - 10, 2 * NU * (e + 1) + s - 9)
                    if s == 0:
                        act.wait_ge(ff1_done, ST * e + 2)
                        w2_part(HC - 1, 0)
                    if s == HC - 1 and not last:
                        act.wait_ge(raw_loaded, 32 * (e + 2))
                    if HC - 1 <= s < 2 * HC - 1 and not last:
                        j = s - (HC - 1)
                        act.wait_ge(ff1_done, ST * e + HC + j + 1)
                        w1_part(j, 0)
                    if s > HC and not last:
                        j = s - HC - 1
                        act.wait_ge(ff2_done, ST * e + HC + j + 1)
                        w2_part(j, 0)
                    if s + 2 < ST or not last:
                        gelu(s + 2, ST * e + s + 2)
                    if s % HC == HC - 1:
                        y_rows(s // HC, e)

            run_experts(act, expert)

        @block.tensor
        def _(pe):
            def turn(dst, src, ident=identf):
                return pe.transpose(dst, src, ident[:])

            pe.wait_ge(consts, 6)
            pe.wait_ge(kv_loaded, 48)
            for dst, src in ((bank[0], ctx_sb), (bank[1], wk_sb)):
                for k in range(KC):
                    for r in range(2):
                        t = turn(dst[:, k * 256 + r * P:k * 256 + (r + 1) * P], src[:, r, k * P:(k + 1) * P])
                t.then_inc(folded, 1)
            pe.wait_ge(ctxT_ready, 1)
            pe.wait_ge(wkT_ready, 1)
            for m in range(KC):
                for k in range(KC):
                    t = pe.matmul((bank[3][:, 0:256], wide[:, 3, 0:256])[m], wkT[:, k, m * P:(m + 1) * P], ctxT[:, k, :],
                                  start=(k == 0), stop=(k == KC - 1))
            t.then_inc(folded, 1)
            pe.wait_ge(q_loaded, 48)
            for k in range(KC):
                t = pe.matmul(wide[:, 2, 0:E], inv_c[:], gate_sb[:, k, :], start=(k == 0), stop=(k == KC - 1))
            t.then_inc(folded, 1)
            pe.wait_ge(v_loaded, 48)
            for k in range(KC):
                for r in range(2):
                    t = turn(bank[2][:, k * 256 + r * P:k * 256 + (r + 1) * P], wv_sb[:, r, k * P:(k + 1) * P])
            t.then_inc(folded, 1)
            pe.wait_ge(kT0_ready, 1)
            pe.wait_ge(kT1_ready, 1)
            for m in range(KC):
                for k in range(KC):
                    t = pe.matmul(wide[:, 0, m * 256:(m + 1) * 256], wq_sb[:, k, m * P:(m + 1) * P], kT[:, k, :],
                                  start=(k == 0), stop=(k == KC - 1))
            t.then_inc(folded, 1)
            for k in range(KC):
                t = pe.matmul(wide[:, 1, 0:B * S], bq_sb[:, k:k + 1].to_broadcast([P, P]), kT[:, k, :],
                              start=(k == 0), stop=(k == KC - 1))
            t.then_inc(folded, 1)
            pe.wait_ge(gate_ready, KC)
            for r in range(KC):
                for k in range(KC):
                    pe.matmul(wide[:, 2, 16 + r * EX:16 + (r + 1) * EX], wv_sb[:, k, r * P:(r + 1) * P],
                              qk[:, k, 0, S:SX], start=(k == 0), stop=(k == KC - 1))
            for k in range(KC):
                t = pe.matmul(wide[0:1, 2, 64:64 + EX], bv_col[:, k:k + 1], qk[:, k, 0, S:SX],
                              start=(k == 0), stop=(k == KC - 1))
            t.then_inc(folded, 1)

            def values():
                pe.wait_ge(wvT_ready, 3)
                pe.wait_ge(qk_ready, 1)
                pe.wait_ge(qk_bias_ready, 1)
                for b in range(B):
                    o = wide[0:S, b, 0:CX]
                    for k in range(KC):
                        pe.matmul(o, ctxT[:, k, b * S:(b + 1) * S], wvT[:, k, :], start=(k == 0), stop=False)
                    t = pe.matmul(o, ones_row[:, 0:S], bv_ext[:], start=False, stop=True)
                t.then_inc(folded, 1)

            def step(j):
                if active(j, 1):
                    g = j - 1
                    pe.wait_ge(xc_ready, g + 1)
                    wait_count(pe, xcT_ready, KC * g)
                    for k in range(KC):
                        for i in range(GT):
                            t = turn(bank[k][:, i * P:(i + 1) * P], xc[:, i, k * P:(k + 1) * P])
                        t.then_inc(xc_turned, 1)
                if active(j, 2):
                    g = j - 2
                    pe.wait_ge(exp_done, g + 1)
                    wait_count(pe, prbT_ready, g)
                    keep_wait(pe, pe_passed)
                    for i in range(GT):
                        t = turn(bank[3][0:S, i * P:(i + 1) * P], prb[:, i, :])
                    t.then_inc(prb_turned, 1)
                if active(j, 1):
                    g = j - 1
                    pe.wait_ge(xcT_ready, KC * (g + 1))
                    if isinstance(g, int) and g == 0:
                        pe.wait_ge(qk_ready, 1)
                    wait_count(pe, max_ready, g)
                    for i in range(GT):
                        for k in range(KC):
                            t = pe.matmul(bank[2][:, i * SX:(i + 1) * SX], xcT[:, k, i * P:(i + 1) * P],
                                          qk[:, k, bass.ds(g // GB, 1), :], start=(k == 0), stop=(k == KC - 1))
                    t.then_inc(scored, 1)
                if active(j, 2):
                    g = j - 2
                    if isinstance(g, int) and g == 0:
                        pe.wait_ge(v_ready, 1)
                    pe.wait_ge(prbT_ready, g + 1)
                    wait_count(pe, x1_ready, GT * g)
                    for i in range(GT):
                        t = pe.matmul(wide[:, i, 0:CX], prbT[:, i * P:(i + 1) * P],
                                      v_sb[:, bass.ds(g // GB, 1), :], start=True, stop=True)
                    t.then_inc(attended, 1)

            run_steps(pe, step, {1: values})

            pe.wait_ge(consts, 13)
            with pe.Fori(0, ROUNDS) as r:
                for h in range(2):
                    pe.wait_ge(over_ready[h], r + 1)
                    for c in range(TC):
                        t = pe.matmul(bank[h][:, 0:HB * KT * E].rearrange("p (b n) -> p b n", b=HB), onesb[:],
                                      over[:, h * HB:(h + 1) * HB, c, :], start=(c == 0), stop=(c == TC - 1))
                    t.then_inc(counted[h], 1)
            pe.wait_ge(masks, 2)

            def shape4(ap):
                return ap.rearrange("p (b c e) -> p b c e", b=B, c=TC)

            def over_all(ap):
                return ap.unsqueeze(2).to_broadcast([P, B, TC, E])

            for dst, m in ((bank[2], above), (bank[3], tied)):
                o = shape4(dst[:, 0:NC * E])
                for c in range(TC):
                    pe.matmul(o, before[:], over_all(m[:, :, c, :]), start=(c == 0), stop=False,
                              skip_group_check=True)
                if m is tied:
                    for c in range(TC):
                        pe.matmul(o, onesb[:], over_all(above[:, :, c, :]), start=False, stop=False,
                                  skip_group_check=True)
                for c in range(TC):
                    t = pe.matmul(o[:, :, c:TC, :], identb[:],
                                  m[:, :, c, :].unsqueeze(2).to_broadcast([P, B, TC - c, E]),
                                  start=False, stop=(c == TC - 1), skip_group_check=True)
                t.then_inc(ranked, 1)

            def list_batch(b, n):
                pe.wait_ge(onehot_ready, n)
                for c in range(TC):
                    t = pe.matmul(bank[3][:, b * LB:(b + 1) * LB], onehot[:, b * TC + c, :], val_e[:, b * TC + c, :],
                                  start=(c == 0), stop=(c == TC - 1))
                t.then_inc(listed, 1)

            def turn_rows(g, k, n, first=False):
                if not first:
                    pe.wait_ge(x_split, n)
                for i in range(NL):
                    t = turn(bank[2][:, i * P:(i + 1) * P], xg[g][:, i, k * P:(k + 1) * P])
                t.then_inc(xg_turned, 1)

            def ff1(s, n, e):
                g, j = s // HC, s % HC
                if j == 0:
                    pe.wait_ge(x_split, 2 * NU * e + 2 * (g + 1))
                if g == 0:
                    pe.wait_ge(w1_split, HC * e + j + 1)
                if not (isinstance(n, int) and n < 2):
                    pe.wait_ge(gelu_done, n - 1)
                m = 0
                for w, xx in ((w1hi, xhi), (w1hi, xlo), (w1lo, xhi)):
                    for k in range(KC):
                        t = pe.matmul(bank[s % 2][:], w[:, j, k, :], xx[g][:, k, :], start=(m == 0), stop=(m == 5))
                        m += 1
                t.then_inc(ff1_done, 1)

            def ff2(s, n, e):
                g, j = s // HC, s % HC
                if g == 0:
                    pe.wait_ge(w2_split, HC * e + j + 1)
                pe.wait_ge(h_split, n + 1)
                for i in range(NL):
                    o = bank[4 + 2 * g + i // 2][:, (i % 2) * C:(i % 2 + 1) * C]
                    for m, (hh, w) in enumerate(((hhi, w2hi), (hhi, w2lo), (hlo, w2hi))):
                        t = pe.matmul(o, hh[s % 4][:, i * P:(i + 1) * P], w[:, j, :],
                                      start=(j == 0 and m == 0 and i % 2 == 0), stop=(j == HC - 1 and m == 2),
                                      skip_group_check=True)
                t.then_inc(ff2_done, 1)

            pe.wait_ge(placed, 2)
            for b in range(B):
                list_batch(b, b + 1)
            pe.wait_ge(gathered[0], 16 * 2 * NL)
            pe.wait_ge(ranked, 2)
            pe.wait_ge(placed, 3)
            for k in range(KC):
                turn_rows(0, k, k, first=(k == 0))
            ff1(0, 0, 0)
            ff1(1, 1, 0)

            def expert(e, last):
                for s in range(ST):
                    if s + 2 < ST:
                        ff1(s + 2, ST * e + s + 2, e)
                    elif not last:
                        ff1(s + 2 - ST, ST * e + s + 2, e + 1)
                    if s == 1:
                        pe.wait_ge(gathered[1], 16 * 2 * NL * (e + 1))
                    if s in (1, 2):
                        turn_rows(1, s - 1, 2 * NU * e + 1 + s)
                    if s == 10 and not last:
                        pe.wait_ge(gathered[0], 16 * 2 * NL * (e + 2))
                    if s in (10, 11) and not last:
                        turn_rows(0, s - 10, 2 * NU * (e + 1) + s - 10)
                    if 1 <= s <= B and not last:
                        list_batch(s - 1, B * (e + 1) + s)
                    ff2(s, ST * e + s, e)

            run_experts(pe, expert)

        @block.vector
        def _(dve):
            dve.wait_ge(folded, 2)
            dve.tensor_copy(wkT[:].rearrange("p k s -> p (k s)"), bank[1][:]).then_inc(wkT_ready, 1)

            def setup():
                dve.wait_ge(folded, 3)
                dve.tensor_scalar(kT[:, 1], wide[:, 3, 0:256], bk_sb[:, 1:2], None, ALU.add).then_inc(kT1_ready, 1)
                dve.wait_ge(folded, 4)
                for k in range(KC):
                    dve.tensor_tensor(qk[:, k, :, S:S + E], gate_sb[:, k].unsqueeze(1).to_broadcast([P, B, E]),
                                      wide[:, 2, 0:E].unsqueeze(1).to_broadcast([P, B, E]),
                                      ALU.subtract).then_inc(gate_ready, 1)
                dve.wait_ge(folded, 7)
                dve.tensor_copy(qk_bias[:].rearrange("p b s -> p (b s)"), wide[:, 1, 0:B * S]).then_inc(qk_bias_ready, 1)

            def step(j):
                if isinstance(j, int) and j < 3:
                    dve.wait_ge((x_first, x_second, x_rest)[j], 16 * (1, 1, B - 1)[j])
                if active(j, 0):
                    g = j
                    wait_count(dve, rstd1, g)
                    keep_wait(dve, dve_passed)
                    for i in range(GT):
                        t = dve.bn_stats(st1[:, i, :], xcols(g)[:, i, :])
                    t.then_inc(stats1, 1)
                    dve.wait_ge(stats1, 2 * g + 1)
                    keep_wait(dve, dve_passed)
                    for i in range(GT):
                        t = dve.bn_aggr(mv1[:, i, :], st1[:, i, :])
                    t.then_inc(stats1, 1)
                    dve.wait_ge(stats1, 2 * g + 2)
                    dve.tensor_scalar(columns_of(nm1, g), mv1[:, :, 0], -1.0, None, ALU.mult).then_inc(mean1, 1)
                    dve.tensor_scalar(ve1[:], mv1[:, :, 1], EPS, None, ALU.add).then_inc(var1, 1)
                if active(j, 3):
                    g = j - 3
                    xcg, ex = xcols(g), columns_of(extra, g)

                    def residual(i):
                        dve.scalar_tensor_tensor(out=xcg[:, i, :], in0=wide[:, i, 0:C], scalar=rinv[:, i:i + 1],
                                                 in1=xcg[:, i, :], op0=ALU.mult, op1=ALU.add).then_inc(x1_ready, 1)

                    dve.wait_ge(attended, g + 1)
                    dve.wait_ge(rinv_ready, g + 1)
                    dve.tensor_tensor(extra_v[:], wide[:, :, C:CX], rinv[:].unsqueeze(2).to_broadcast([P, GT, EX]),
                                      ALU.mult).then_inc(extra_ready, 1)
                    residual(0)
                    dve.wait_ge(extra_ready, 3 * g + 1)
                    dve.tensor_tensor(ex, ex, extra_v[:], ALU.add).then_inc(extra_ready, 1)
                    residual(1)
                    dve.wait_ge(extra_ready, 3 * g + 2)
                    dve.scalar_tensor_tensor(out=columns_of(nm2, g).unsqueeze(2), in0=ex[:, :, E:EX], scalar=-1.0,
                                             in1=columns_of(nm1, g).unsqueeze(2),
                                             op0=ALU.mult, op1=ALU.add).then_inc(extra_ready, 1)
                    residual(2)
                    residual(3)
                if active(j, 1):
                    g = j - 1
                    dve.wait_ge(scored, g + 1)
                    dve.wait_ge(rstd1, g + 1)
                    if isinstance(g, int) and g == 0:
                        dve.wait_ge(qk_bias_ready, 1)
                    for i in range(GT):
                        t = dve.scalar_tensor_tensor(out=score[:, i, :], in0=bank[2][:, i * SX:i * SX + S],
                                                     scalar=rs1[:, i:i + 1],
                                                     in1=qk_bias[:, bass.ds(g // GB, 1), :].rearrange("p b s -> p (b s)"),
                                                     op0=ALU.mult, op1=ALU.add)
                    t.then_inc(score_ready, 1)
                    dve.tensor_copy(columns_of(extra, g),
                                    bank[2][:, 0:GT * SX].rearrange("p (i s) -> p i s", i=GT)[:, :, S:SX])
                if active(j, 2):
                    g = j - 2
                    dve.wait_ge(exp_done, g + 1)
                    wait_count(dve, x1_ready, GT * g)
                    dve.reciprocal(rinv[:], psums[:]).then_inc(rinv_ready, 1)
                if active(j, 1):
                    g = j - 1
                    dve.wait_ge(score_ready, g + 1)
                    dve.tensor_reduce(nmax[:], score[:], AX.X, ALU.max, negate=True).then_inc(max_ready, 1)

            run_steps(dve, step, {0: setup})

            dve.wait_ge(squared, NC)
            dve.tensor_scalar(ve2[:], ss2[:], 1.0 / C, EPS, ALU.mult, ALU.add).then_inc(ve2_ready, 1)
            logits = extra[:, :, 0:E]
            pr = prob[:].rearrange("p b c e -> p (b c) e")
            dve.wait_ge(rstd2, 1)
            dve.tensor_tensor(nb2[:], nm2[:], rs2[:], ALU.mult).then_inc(nb2_ready, 1)
            dve.tensor_tensor(logits, logits, rs2[:].unsqueeze(2).to_broadcast([P, NC, E]), ALU.mult).then_inc(soft, 1)
            dve.wait_ge(soft, 1)
            dve.tensor_reduce(gmax[:], logits, AX.X, ALU.max).then_inc(soft, 1)
            dve.wait_ge(soft, 2)
            dve.tensor_tensor(pr, logits, gmax[:].unsqueeze(2).to_broadcast([P, NC, E]), ALU.subtract).then_inc(soft, 1)
            dve.wait_ge(gexp, 1)
            dve.tensor_reduce(gsum[:], pr, AX.X, ALU.add).then_inc(soft, 1)
            dve.wait_ge(soft, 4)
            dve.reciprocal(gmax[:], gsum[:]).then_inc(soft, 1)
            dve.wait_ge(soft, 5)
            dve.tensor_tensor(pr, pr, gmax[:].unsqueeze(2).to_broadcast([P, NC, E]), ALU.mult).then_inc(soft, 1)

            dve.wait_ge(consts, 13)

            def half(ap, h):
                return ap[:, h * HB:(h + 1) * HB]

            for h in range(2):
                dve.tensor_scalar(half(cand_off, h), half(cand_off, h), BITS - RB, None,
                                  ALU.logical_shift_left).then_inc(off_ready[h], 1)
                dve.tensor_copy(half(reached, h)[:, :, KT, :], half(floor_, h)).then_inc(floor_set, 1)
            dve.wait_ge(soft, 6)

            def compare(h, n):
                dve.wait_ge(off_ready[h], n + 1)
                dve.tensor_tensor(half(cand, h), half(floor_, h).bitcast(I32).unsqueeze(2).to_broadcast([P, HB, KT, E]),
                                  half(cand_off, h), ALU.bitwise_or).then_inc(cand_ready[h], 1)
                dve.wait_ge(cand_ready[h], n + 1)
                for b in range(HB):
                    t = dve.tensor_tensor(
                        half(over, h)[:, b].rearrange("p c (k e) -> p c k e", k=KT),
                        half(prob, h)[:, b].unsqueeze(2).to_broadcast([P, TC, KT, E]),
                        half(cand, h)[:, b].bitcast(F32).unsqueeze(1).to_broadcast([P, TC, KT, E]), ALU.is_ge)
                t.then_inc(over_ready[h], 1)
                dve.tensor_scalar(half(cand_off, h), half(cand_off, h), RB, None,
                                  ALU.logical_shift_right).then_inc(off_ready[h], 1)

            def settle(h, n):
                dve.wait_ge(counted[h], n + 1)
                dve.scalar_tensor_tensor(out=half(reached, h)[:, :, 0:KT, :].rearrange("p b k e -> p b (k e)"),
                                         in0=bank[h][:, 0:HB * KT * E].rearrange("p (b n) -> p b n", b=HB),
                                         scalar=float(CAP),
                                         in1=half(cand, h).bitcast(F32).rearrange("p b k e -> p b (k e)"),
                                         op0=ALU.is_ge, op1=ALU.mult).then_inc(reached_ready[h], 1)
                dve.wait_ge(reached_ready[h], n + 1)
                dve.tensor_reduce(half(floor_, h), half(reached, h).rearrange("p b k e -> p b e k"), AX.X,
                                  ALU.max).then_inc(floor_ready[h], 1)
                dve.wait_ge(floor_ready[h], n + 1)

            dve.wait_ge(floor_set, 2)
            compare(0, 0)
            compare(1, 0)

            UR = 2
            with dve.Fori(0, (ROUNDS - 1) // UR) as r:
                for i in range(UR):
                    for h in range(2):
                        settle(h, r * UR + i)
                        dve.tensor_copy(half(reached, h)[:, :, KT, :], half(floor_, h)).then_inc(floor_set, 1)
                        compare(h, r * UR + i + 1)
            for h in range(2):
                settle(h, ROUNDS - 1)

            for b in range(B):
                f = floor_[:, b].unsqueeze(1).to_broadcast([P, TC, E])
                t = dve.tensor_tensor(above[:, b], prob[:, b], f, ALU.is_gt)
            t.then_inc(masks, 1)
            for b in range(B):
                f = floor_[:, b].unsqueeze(1).to_broadcast([P, TC, E])
                t = dve.tensor_tensor(tied[:, b], prob[:, b], f, ALU.is_equal)
            t.then_inc(masks, 1)

            def flat(ap):
                return ap.rearrange("p b c e -> p (b c e)")

            dve.wait_ge(masks, 2)
            dve.wait_ge(ranked, 1)
            dve.tensor_tensor(flat(pos_a[:]), bank[2][:, 0:NC * E], flat(above[:]), ALU.mult).then_inc(placed, 1)
            dve.wait_ge(ranked, 2)
            dve.tensor_tensor(flat(pos_t[:]), bank[3][:, 0:NC * E], flat(tied[:]), ALU.mult).then_inc(placed, 1)
            dve.wait_ge(placed, 2)
            dve.tensor_tensor(pos_a[:], pos_a[:], pos_t[:], ALU.add).then_inc(placed, 1)
            dve.wait_ge(placed, 3)
            dve.tensor_scalar(second[:], pos_a[:], P + 0.5, None, ALU.is_gt).then_inc(placed, 1)
            dve.wait_ge(placed, 4)
            sl = slot_of[:].rearrange("p n e -> p (n e)")
            dve.scalar_tensor_tensor(out=sl, in0=flat(second[:]), scalar=-float(P), in1=flat(pos_a[:]),
                                     op0=ALU.mult, op1=ALU.add).then_inc(placed, 1)
            dve.tensor_tensor(pos_t[:], second[:], tok_no[:], ALU.mult).then_inc(placed, 1)
            dve.wait_ge(placed, 6)
            tv = tok_val[:].rearrange("p n e l -> p (n e) l")
            dve.tensor_copy(tv[:, :, 1], flat(pos_t[:])).then_inc(placed, 1)
            dve.tensor_tensor(tv[:, :, 0], flat(tok_no[:]), flat(pos_t[:]), ALU.subtract).then_inc(placed, 1)
            dve.wait_ge(placed, 8)

            def columns(e, n):
                dve.tensor_copy(slot_e[:].unsqueeze(2), slot_of[:, :, bass.ds(e, 1)]).then_inc(col_ready, 1)
                dve.tensor_copy(val_e[:].unsqueeze(2), tok_val[:, :, bass.ds(e, 1), :]).then_inc(col_ready, 1)
                dve.wait_ge(col_ready, n)

            def one_hot(b):
                for c in range(TC):
                    t = dve.tensor_scalar(onehot[:, b * TC + c, :], slot_no[:], slot_e[:, b * TC + c:b * TC + c + 1],
                                          None, ALU.is_equal)
                t.then_inc(onehot_ready, 1)

            def index_list(n):
                dve.wait_ge(listed, B * n)
                dve.tensor_tensor(gidx[:], bank[3][:, 0:B * LB], row0[:], ALU.add).then_inc(gidx_ready, 1)

            def x_rest_part(g, k, n):
                dve.wait_ge(x_hi, n)
                dve.tensor_tensor(xlo[g][:, k], bank[2][:], xhi[g][:, k].bitcast(F32), ALU.subtract).then_inc(x_split, 1)

            def prob_column(g, e):
                dve.tensor_copy(pcol[g][:].unsqueeze(2), pg[g][:, :, bass.ds(e, 1)]).then_inc(pcol_ready, 1)

            def split_h(s, n):
                dve.wait_ge(gelu_done, n + 1)
                dve.tensor_copy(hhi[s % 4][:], hraw[s % 2][:]).then_inc(h_hi, 1)
                dve.wait_ge(h_hi, n + 1)
                dve.tensor_tensor(hlo[s % 4][:], hraw[s % 2][:], hhi[s % 4][:].bitcast(F32),
                                  ALU.subtract).then_inc(h_split, 1)

            dve.wait_ge(first_split, 2 * HC - 1)
            dve.sem_inc(w1_split, HC)
            dve.sem_inc(w2_split, HC - 1)

            columns(0, 2)
            for b in range(B):
                one_hot(b)
            index_list(1)
            for k in range(KC):
                x_rest_part(0, k, k + 1)
            dve.wait_ge(gathered[0], 16 * 2 * NL)
            prob_column(0, 0)
            split_h(0, 0)
            split_h(1, 1)

            def expert(e, last):
                for s in range(ST):
                    if s == 0:
                        dve.wait_ge(w2_hi, HC * (e + 1))
                        dve.tensor_tensor(w2lo[:, HC - 1], w2raw[:, HC - 1], w2hi[:, HC - 1].bitcast(F32),
                                          ALU.subtract).then_inc(w2_split, 1)
                        if not last:
                            columns(e + 1, 2 * (e + 2))
                    if s in (1, 2):
                        x_rest_part(1, s - 1, 2 * NU * e + 2 + s)
                    if s == 2:
                        dve.wait_ge(gathered[1], 16 * 2 * NL * (e + 1))
                        prob_column(1, e)
                    if s < B and not last:
                        one_hot(s)
                    if s == 4:
                        dve.wait_ge(settled, e + 1)
                        dve.tensor_copy(sidx[:], gidx[:]).then_inc(sidx_ready, 1)
                    if s == 5 and not last:
                        dve.wait_ge(sidx_ready, e + 1)
                        index_list(e + 2)
                    if s in (10, 11) and not last:
                        x_rest_part(0, s - 10, 2 * NU * (e + 1) + s - 9)
                    if s == 11 and not last:
                        dve.wait_ge(gathered[0], 16 * 2 * NL * (e + 2))
                        dve.wait_ge(y_ready, 2 * e + 1)
                        prob_column(0, e + 1)
                    if HC - 1 <= s < 2 * HC - 1 and not last:
                        j = s - (HC - 1)
                        dve.wait_ge(w1_hi, HC * (e + 1) + j + 1)
                        dve.tensor_tensor(w1lo[:, j], w1raw[:, :, bass.ts(j, P)], w1hi[:, j].bitcast(F32),
                                          ALU.subtract).then_inc(w1_split, 1)
                    if s > HC and not last:
                        j = s - HC - 1
                        dve.wait_ge(w2_hi, HC * (e + 1) + j + 1)
                        dve.tensor_tensor(w2lo[:, j], w2raw[:, j], w2hi[:, j].bitcast(F32),
                                          ALU.subtract).then_inc(w2_split, 1)
                    if s + 2 < ST or not last:
                        split_h(s + 2, ST * e + s + 2)

            run_experts(dve, expert)


_INS = ['x', 'ctx_1024', 'L0_xattn_Wq', 'L0_xattn_bq', 'L0_xattn_Wk', 'L0_xattn_bk', 'L0_xattn_Wv', 'L0_xattn_bv',
        'L0_ffn_gate_w', 'L0_ffn_w1', 'L0_ffn_w2']


def kernel(**inputs):
    import numpy as _np
    import concourse.bacc as _bacc
    from concourse import mybir as _mybir
    from concourse.bass_utils import run_bass_kernel_spmd as _run

    nc = _bacc.Bacc("TRN2", target_bir_lowering=False, num_devices=1)
    arrays, args = {}, []
    for name in _INS:
        a = _np.ascontiguousarray(inputs[name])
        arrays[f"in_{name}_dram"] = a
        args.append(nc.dram_tensor(f"in_{name}_dram", a.shape, _mybir.dt.from_np(a.dtype), kind="ExternalInput").ap())
    args.append(nc.dram_tensor("out_0_dram", inputs['x'].shape, _mybir.dt.float32, kind="ExternalOutput").ap())
    build(nc, *args)
    r = _run(nc, [arrays], core_ids=[0])
    return r.results[0]["out_0_dram"]
```

```python
from contextlib import ExitStack

import concourse.bass as bass
from concourse import mybir

F32 = mybir.dt.float32
F32R = mybir.dt.float32r
F16 = mybir.dt.float16
I32 = mybir.dt.int32
I16 = mybir.dt.int16
ALU = mybir.AluOpType
ACT = mybir.ActivationFunctionType
AX = mybir.AxisListType

P = 128
EPS = 1e-5


def wait_count(eng, sem, n):
    if isinstance(n, int) and n <= 0:
        return
    eng.wait_ge(sem, n)


def build(nc, x, ctx_in, Wq, bq, Wk, bk, Wv, bv, gate_w, w1, w2, out):
    B, T, C = x.shape
    S = ctx_in.shape[1]
    E, _, H = w1.shape
    CAP = 2 * T // E
    TC = T // P
    NC = B * TC
    KC = C // P
    HC = H // P
    GT = 4
    NG = NC // GT
    GB = TC // GT
    LB = CAP // P
    UB = 2
    NU = B // UB
    NL = UB * LB
    UT = NL * P
    ST = NU * HC
    BITS, RB = 15, 3
    KT = 2 ** RB - 1
    ROUNDS = BITS // RB
    HB = B // 2
    EX = E + 1
    SX = S + EX
    CX = C + EX
    assert UB == HB and NU == 2
    assert KC == 2 and UT == 512 and B * S == 2 * P and NC * E == 256

    xn_dram = nc.dram_tensor("xn_rows", (B * T, C), F32, kind="Internal").ap()
    pr_dram = nc.dram_tensor("prob_rows", (B * T, E), F32, kind="Internal").ap()

    x_v = x.rearrange("b (p c) d -> b p c d", c=TC)
    out_v = out.rearrange("b (p c) d -> p b c d", c=TC)
    xn_v = xn_dram.rearrange("(b p c) d -> p b c d", b=B, c=TC)
    pr_v = pr_dram.rearrange("(b p c) e -> p b (c e)", b=B, c=TC)
    out_rows = out.rearrange("b t d -> (b t) d")

    with ExitStack() as stack:
        def sb(name, shape, dt):
            return stack.enter_context(nc.sbuf_tensor(name, shape, dt))

        def sem(name):
            return stack.enter_context(nc.semaphore(name))

        bank = [stack.enter_context(nc.psum_tensor(f"bank{i}", [P, 512], F32)) for i in range(4)]
        wide = stack.enter_context(nc.psum_tensor("wide", [P, 4, 512], F32))
        bank += [wide[:, i] for i in range(4)]

        identf = sb("identf", [P, P], F32)
        onesb = sb("onesb", [P, P], F16)
        before = sb("before", [P, P], F16)
        ones_row = sb("ones_row", [1, P], F32)
        slot_no = sb("slot_no", [P, P, TC], F16)
        tok_no = sb("tok_no", [P, B, E, TC], F16)
        warm = sb("warm", [P, 1], F32)
        go_on = sb("go_on", [P, HB, E, TC], F16)
        row0 = sb("row0", [P, B * LB], F32)
        neghalf = sb("neghalf", [P, NC], F32)
        inv_c = sb("inv_c", [P, P], F32)
        step_wide = sb("step_wide", [P, ROUNDS, KT + 1, E], I32)
        step_bits = sb("step_bits", [P, ROUNDS, KT + 1, E], I16)
        wk_sb = sb("wk_sb", [P, KC, C], F32)
        wq_sb = sb("wq_sb", [P, KC, C], F32)
        wv_sb = sb("wv_sb", [P, KC, C], F32)
        ctx_sb = sb("ctx_sb", [P, KC, C], F32)
        bk_sb = sb("bk_sb", [P, KC], F32)
        bq_sb = sb("bq_sb", [P, KC], F32)
        bv_ext = sb("bv_ext", [1, CX], F32)
        bv_col = sb("bv_col", [P, KC], F32)
        gate_sb = sb("gate_sb", [P, KC, E], F32)
        ctxT = sb("ctxT", [P, KC, B * S], F32)
        wkT = sb("wkT", [P, KC, C], F32)
        wvT = sb("wvT", [P, KC, CX], F32)
        kT = sb("kT", [P, KC, B * S], F32)
        qk = sb("qk", [P, KC, B, SX], F32)
        qk_bias = sb("qk_bias", [P, B, S], F32)
        v_sb = sb("v_sb", [S, B, CX], F32)
        v_odd = sb("v_odd", [P, B // 2, CX], F32)
        x_all = sb("x_all", [P, B, TC, C], F32)
        st1 = sb("st1", [P, GT, 6], F32)
        mv1 = sb("mv1", [P, GT, 2], F32)
        ve1 = sb("ve1", [P, NC], F32)
        rs1 = sb("rs1", [P, NC], F32)
        nm1 = sb("nm1", [P, NC], F32)
        xc = sb("xc", [P, GT, C], F32)
        xcT = sb("xcT", [P, KC, GT * P], F32)
        score = sb("score", [P, GT, S], F32)
        nmax = sb("nmax", [P, GT], F32)
        prb = sb("prb", [P, GT, S], F32)
        psums = sb("psums", [P, GT], F32)
        prbT = sb("prbT", [S, GT * P], F32)
        rinv = sb("rinv", [P, GT], F32)
        extra = sb("extra", [P, NC, EX], F32)
        extra_v = sb("extra_v", [P, GT, EX], F32)
        nm2 = sb("nm2", [P, NC], F32)
        sq = sb("sq", [P, GT, C], F32)
        ss2 = sb("ss2", [P, NC], F32)
        ve2 = sb("ve2", [P, NC], F32)
        rs2 = sb("rs2", [P, NC], F32)
        nb2 = sb("nb2", [P, NC], F32)
        gmax = sb("gmax", [P, NC], F32)
        gsum = sb("gsum", [P, NC], F32)
        prob = sb("prob", [P, B, TC, E], F32)
        upper = sb("upper", [P, B, TC, E], I32)
        lower = sb("lower", [P, B, TC, E], I32)
        key = sb("key", [P, B, TC, E], I16)
        above_found = sb("above_found", [P, B, TC, E], F32)
        floor_ = sb("floor", [P, B, E], I16)
        found = sb("found", [P, B, E], I32)
        last_bits = sb("last_bits", [P, B, E], I32)
        cand = sb("cand", [P, B, KT + 1, E], I16)
        over = sb("over", [P, B, TC, KT * E], F16)
        reached = sb("reached", [P, B, KT + 1, E], I16)
        mask = [sb(f"mask{h}", [P, 2, HB, E, TC], F16) for h in range(2)]
        upto = [sb(f"upto{h}", [P, 2, HB, E, TC], F16) for h in range(2)]
        place = [sb(f"place{h}", [P, 2, HB, E, TC], F16) for h in range(2)]
        slot_any = sb("slot_any", [P, B, E, TC], F16)
        second = sb("second", [P, B, E, TC], F16)
        slot_of = sb("slot_of", [P, B, E, TC], F16)
        tok_val = sb("tok_val", [P, B, E, LB, TC], F16)
        onehot = sb("onehot", [P, B, P, TC], F16)
        gidx = sb("gidx", [P, B * LB], I32)
        sidx = sb("sidx", [P, B * LB], I32)
        w1raw = sb("w1raw", [P, KC, H], F32)
        w2raw = sb("w2raw", [P, HC, C], F32)
        w1hi = sb("w1hi", [P, HC, KC, P], F32R)
        w1lo = sb("w1lo", [P, HC, KC, P], F32R)
        w2hi = sb("w2hi", [P, HC, C], F32R)
        w2lo = sb("w2lo", [P, HC, C], F32R)
        xg = [sb(f"xg{g}", [P, NL, C], F32) for g in range(NU)]
        pg = [sb(f"pg{g}", [P, NL, E], F32) for g in range(NU)]
        pcol = [sb(f"pcol{g}", [P, NL], F32) for g in range(NU)]
        xhi = [sb(f"xhi{g}", [P, KC, UT], F32R) for g in range(NU)]
        xlo = [sb(f"xlo{g}", [P, KC, UT], F32R) for g in range(NU)]
        hraw = [sb(f"hraw{i}", [P, UT], F32) for i in range(2)]
        hhi = [sb(f"hhi{i}", [P, UT], F32R) for i in range(4)]
        hlo = [sb(f"hlo{i}", [P, UT], F32R) for i in range(4)]
        ysb = [sb(f"ysb{g}", [P, NL, C], F32) for g in range(NU)]

        kv_loaded = sem("kv_loaded")
        q_loaded = sem("q_loaded")
        v_loaded = sem("v_loaded")
        x_first = sem("x_first")
        x_second = sem("x_second")
        x_rest = sem("x_rest")
        consts = sem("consts")
        bits_set = sem("bits_set")
        folded = sem("folded")
        ctxT_ready = sem("ctxT_ready")
        wkT_ready = sem("wkT_ready")
        kT0_ready = sem("kT0_ready")
        kT1_ready = sem("kT1_ready")
        gate_ready = sem("gate_ready")
        qk_ready = sem("qk_ready")
        qk_bias_ready = sem("qk_bias_ready")
        wvT_ready = sem("wvT_ready")
        v_ready = sem("v_ready")
        v_moved = sem("v_moved")
        stats1 = sem("stats1")
        mean1 = sem("mean1")
        var1 = sem("var1")
        rstd1 = sem("rstd1")
        xc_ready = sem("xc_ready")
        xc_turned = sem("xc_turned")
        xcT_ready = sem("xcT_ready")
        scored = sem("scored")
        score_ready = sem("score_ready")
        max_ready = sem("max_ready")
        exp_done = sem("exp_done")
        prb_turned = sem("prb_turned")
        prbT_ready = sem("prbT_ready")
        attended = sem("attended")
        rinv_ready = sem("rinv_ready")
        extra_ready = sem("extra_ready")
        x1_ready = sem("x1_ready")
        squared = sem("squared")
        ve2_ready = sem("ve2_ready")
        rstd2 = sem("rstd2")
        nb2_ready = sem("nb2_ready")
        xn2_ready = sem("xn2_ready")
        rows_stored = sem("rows_stored")
        rows_added = sem("rows_added")
        settled = sem("settled")
        xn_stored = sem("xn_stored")
        soft = sem("soft")
        gexp = sem("gexp")
        pr_stored = sem("pr_stored")
        bits_ready = sem("bits_ready")
        key_parts = sem("key_parts")
        key_ready = sem("key_ready")
        found_ready = [sem(f"found_ready{h}") for h in range(2)]
        cand_ready = [sem(f"cand_ready{h}") for h in range(2)]
        over_ready = [[sem(f"over_ready{h}_{b}") for b in range(HB)] for h in range(2)]
        counted = [sem(f"counted{h}") for h in range(2)]
        reached_ready = [sem(f"reached_ready{h}") for h in range(2)]
        floor_ready = [sem(f"floor_ready{h}") for h in range(2)]
        masks = [sem(f"masks{h}") for h in range(2)]
        summed = [sem(f"summed{h}") for h in range(2)]
        ranked = [sem(f"ranked{h}") for h in range(2)]
        placed = [sem(f"placed{h}") for h in range(2)]
        onehot_ready = [sem(f"onehot_ready{b}") for b in range(B)]
        listed = [sem(f"listed{h}") for h in range(2)]
        gidx_ready = [sem(f"gidx_ready{h}") for h in range(2)]
        sidx_ready = sem("sidx_ready")
        raw_loaded = sem("raw_loaded")
        w1_hi = sem("w1_hi")
        w2_hi = sem("w2_hi")
        first_split = sem("first_split")
        w1_split = sem("w1_split")
        w2_split = sem("w2_split")
        gathered = [sem(f"gathered{g}") for g in range(NU)]
        prob_gathered = [sem(f"prob_gathered{g}") for g in range(NU)]
        xg_turned = sem("xg_turned")
        x_hi = sem("x_hi")
        x_split = sem("x_split")
        pcol_ready = sem("pcol_ready")
        ff1_done = sem("ff1_done")
        gelu_done = sem("gelu_done")
        h_hi = sem("h_hi")
        h_split = sem("h_split")
        ff2_done = sem("ff2_done")
        bank_done = sem("bank_done")
        y_ready = sem("y_ready")

        dve_passed = sem("dve_passed")
        pe_passed = sem("pe_passed")
        pool_passed = sem("pool_passed")

        def keep_wait(eng, passed):
            eng.sem_inc(passed, 1)

        LAST = 4

        N_CONST = 13

        def active(j, stage):
            return not isinstance(j, int) or 0 <= j - stage < NG

        def run_steps(eng, body, after={}):
            for j in range(LAST + 1):
                body(j)
                if j in after:
                    after[j]()
            with eng.Fori(LAST + 1, NG) as j:
                body(j)
            for j in range(NG, NG + LAST):
                body(j)
                if j in after:
                    after[j]()

        def counts(h):
            return bank[h][:, 0:HB * (KT + 1) * E].rearrange("p (b n) -> p b n", b=HB)

        def half(ap, h):
            return ap[:, h * HB:(h + 1) * HB]

        def columns_of(ap, g):
            return ap[:, bass.ts(g, GT)]

        def xcols(g):
            return x_all[:].rearrange("p b c d -> p (b c) d")[:, bass.ts(g, GT), :]

        def run_experts(eng, body):
            with eng.Fori(0, E - 1) as e:
                body(e, False)
            body(E - 1, True)

        block = stack.enter_context(nc.Block())

        @block.sync
        def _(sp):
            x_g = x.rearrange("b (p q c) d -> p b q (c d)", q=GB, c=GT)
            sp.dma_start(wk_sb[:], Wk.rearrange("(k p) d -> p k d", p=P)).then_inc(kv_loaded, 16)
            sp.dma_start(ctx_sb[:], ctx_in.rearrange("b s d -> (b s) d").rearrange("(k p) d -> p k d", p=P)).then_inc(kv_loaded, 16)
            sp.dma_start(bk_sb[:], bk.rearrange("(k p) -> p k", p=P), allow_slow_non_contiguous=True).then_inc(kv_loaded, 16)
            sp.dma_start(xcols(0), x_g[:, 0, 0]).then_inc(x_first, 16)
            sp.dma_start(wq_sb[:], Wq.rearrange("(k p) d -> p k d", p=P)).then_inc(q_loaded, 16)
            sp.dma_start(bq_sb[:], bq.rearrange("(k p) -> p k", p=P), allow_slow_non_contiguous=True).then_inc(q_loaded, 16)
            sp.dma_start(gate_sb[:], gate_w.rearrange("(k p) e -> p k e", p=P)).then_inc(q_loaded, 16)
            sp.dma_start(xcols(1), x_g[:, 0, 1]).then_inc(x_second, 16)
            sp.dma_start(wv_sb[:], Wv.rearrange("(k p) d -> p k d", p=P)).then_inc(v_loaded, 16)
            sp.dma_start(bv_ext[:, 0:C], bv.rearrange("(a d) -> a d", a=1)).then_inc(v_loaded, 16)
            sp.dma_start(bv_col[:], bv.rearrange("(k p) -> p k", p=P), allow_slow_non_contiguous=True).then_inc(v_loaded, 16)
            for b in range(1, B):
                sp.dma_start(x_all[:, b], x_v[b]).then_inc(x_rest, 16)
            sp.dma_start(w1raw[:], w1[0].rearrange("(k p) h -> p k h", p=P)).then_inc(raw_loaded, 16)
            sp.dma_start(w2raw[:], w2[0].rearrange("(k p) d -> p k d", p=P)).then_inc(raw_loaded, 16)

            out_g = out.rearrange("b (p q c) d -> p b q (c d)", q=GB, c=GT)

            def step(j):
                if active(j, 4):
                    g = j - 4
                    sp.wait_ge(x1_ready, GT * (g + 1))
                    sp.dma_start(out_g[:, g // GB, g % GB], xcols(g)).then_inc(rows_stored, 16)

            def odd_values():
                sp.wait_ge(v_ready, 2)
                sp.dma_start(v_sb[:, 1:B:2, :], v_odd[S:P]).then_inc(v_moved, 16)

            run_steps(sp, step, {2: odd_values})
            for b in range(B):
                sp.wait_ge(xn2_ready, GB * (b + 1))
                sp.dma_start(xn_v[:, b], x_all[:, b]).then_inc(xn_stored, 16)
            sp.wait_ge(soft, 6)
            sp.dma_start(pr_v, prob[:].rearrange("p b c e -> p b (c e)")).then_inc(pr_stored, 16)

            def load_next(e, last):
                if not last:
                    sp.wait_ge(w2_split, HC * (e + 1))
                    sp.dma_start(w1raw[:], w1_v[:, e + 1]).then_inc(raw_loaded, 16)
                    sp.dma_start(w2raw[:], w2_v[:, e + 1]).then_inc(raw_loaded, 16)

            w1_v = w1.rearrange("e (k p) h -> p e k h", p=P)
            w2_v = w2.rearrange("e (k p) d -> p e k d", p=P)
            run_experts(sp, load_next)

        @block.gpsimd
        def _(pool):
            pool.memset(identf[:], 0.0).then_inc(bits_set, 1)
            pool.memset(before[:], 1.0).then_inc(bits_set, 1)
            pool.memset(ones_row[:], 1.0).then_inc(consts, 1)
            pool.memset(inv_c[:], 1.0 / C).then_inc(consts, 1)
            pool.memset(qk[:, :, :, SX - 1:SX], 1.0 / C).then_inc(consts, 1)
            pool.memset(neghalf[:], -0.5).then_inc(consts, 1)
            pool.memset(go_on[:], 1.0).then_inc(bits_set, 1)
            pool.wait_ge(bits_set, 3)
            pool.affine_select(out=identf[:], in_=identf[:], compare_op=ALU.not_equal, fill=1.0, base=0,
                               pattern=[[-1, P]], channel_multiplier=1).then_inc(consts, 1)
            pool.affine_select(out=before[:], in_=before[:], compare_op=ALU.is_gt, fill=0.0, base=0,
                               pattern=[[1, P]], channel_multiplier=-1).then_inc(consts, 1)
            pool.memset(onesb[:], 1.0).then_inc(consts, 1)
            pool.memset(floor_[:], 0).then_inc(consts, 1)
            pool.memset(go_on[:, :, :, 0:1], 0.0).then_inc(consts, 1)
            pool.iota(step_wide[:], [[0, ROUNDS], [1, KT + 1], [0, E]], base=0, channel_multiplier=0).then_inc(consts, 1)
            pool.iota(slot_no[:], [[1, P], [0, TC]], base=1, channel_multiplier=0,
                      allow_small_or_imprecise_dtypes=True).then_inc(consts, 1)
            pool.iota(tok_no[:], [[0, B * E], [1, TC]], base=0, channel_multiplier=TC,
                      allow_small_or_imprecise_dtypes=True).then_inc(consts, 1)
            pool.iota(row0[:], [[T, B], [0, LB]], base=0, channel_multiplier=0,
                      allow_small_or_imprecise_dtypes=True).then_inc(consts, 1)

            pool.wait_ge(consts, N_CONST)

            def step(j):
                if active(j, 0):
                    g = j
                    wait_count(pool, xc_turned, KC * g)
                    pool.wait_ge(mean1, g + 1)
                    pool.tensor_tensor(xc[:], xcols(g), columns_of(nm1, g).unsqueeze(2).to_broadcast([P, GT, C]),
                                       ALU.add).then_inc(xc_ready, 1)
                    pool.wait_ge(var1, g + 1)
                    pool.tensor_tensor(columns_of(rs1, g), columns_of(ve1, g), neghalf[:, 0:GT],
                                       ALU.pow).then_inc(rstd1, 1)

            def factors(lo, hi, n):
                pool.wait_ge(ve2_ready, n)
                pool.tensor_tensor(rs2[:, lo:hi], ve2[:, lo:hi], neghalf[:, lo:hi], ALU.pow).then_inc(rstd2, 1)

            run_steps(pool, step, {NG + 1: lambda: factors(0, NC - 3 * GT, 1),
                                   NG + 2: lambda: factors(NC - 3 * GT, NC - GT, 2)})
            factors(NC - GT, NC, 3)

            for j in range(HC):
                pool.wait_ge(w1_hi, j + 1)
                pool.tensor_tensor(w1lo[:, j], w1raw[:, :, bass.ts(j, P)], w1hi[:, j].bitcast(F32),
                                   ALU.subtract).then_inc(first_split, 1)
            for j in range(HC - 1):
                pool.wait_ge(w2_hi, j + 1)
                pool.tensor_tensor(w2lo[:, j], w2raw[:, j], w2hi[:, j].bitcast(F32),
                                   ALU.subtract).then_inc(first_split, 1)

            def gather_to(dst, rows, g, done):
                for i in range(NL):
                    at = bass.IndirectOffsetOnAxis(ap=gidx[:, g * NL + i:g * NL + i + 1], axis=0)
                    pool.indirect_dma_start(out=dst[g][:, i, :], out_offset=None, in_=rows,
                                            in_offset=at).then_inc(done[g], 16)

            def gather(g):
                keep_wait(pool, pool_passed)
                gather_to(xg, xn_dram, g, gathered)
                gather_to(pg, pr_dram, g, prob_gathered)

            def scatter(g, e):
                for i in range(NL):
                    pool.wait_ge(y_ready, NL * (NU * e + g) + i + 1)
                    keep_wait(pool, pool_passed)
                    at = bass.IndirectOffsetOnAxis(ap=sidx[:, g * NL + i:g * NL + i + 1], axis=0)
                    pool.indirect_dma_start(out=out_rows, out_offset=at, in_=ysb[g][:, i, :], in_offset=None,
                                            compute_op=ALU.add).then_inc(rows_added, 16)

            pool.wait_ge(xn_stored, 16 * B)
            pool.wait_ge(pr_stored, 16)
            for g in range(NU):
                pool.wait_ge(gidx_ready[g], 1)
                gather_to(xg, xn_dram, g, gathered)
            for g in range(NU):
                gather_to(pg, pr_dram, g, prob_gathered)

            def expert(e, last):
                if not last:
                    for g in range(NU):
                        pool.wait_ge(gidx_ready[g], e + 2)
                    pool.wait_ge(xg_turned, 2 * NU * e + 4)
                    gather(0)
                pool.wait_ge(sidx_ready, e + 1)
                scatter(0, e)
                if not last:
                    pool.wait_ge(pcol_ready, 2 * e + 2)
                    gather(1)
                scatter(1, e)
                pool.wait_ge(rows_added, 16 * NU * NL * (e + 1))
                pool.sem_inc(settled, 1)

            pool.wait_ge(rows_stored, 16 * NG)
            pool.sem_inc(settled, 1)
            run_experts(pool, expert)

        @block.scalar
        def _(act):
            act.wait_ge(folded, 1)
            act.activation(ctxT[:].rearrange("p k s -> p (k s)"), bank[0][:], ACT.Copy).then_inc(ctxT_ready, 1)

            def setup():
                act.wait_ge(kv_loaded, 48)
                act.wait_ge(folded, 3)
                act.activation(kT[:, 0], bank[3][:, 0:256], ACT.Identity, bias=bk_sb[:, 0:1]).then_inc(kT0_ready, 1)
                act.wait_ge(folded, 5)
                act.activation(wvT[:, :, 0:C], bank[2][:].rearrange("p (k s) -> p k s", k=KC), ACT.Copy).then_inc(wvT_ready, 1)

            def folded_keys():
                act.wait_ge(folded, 6)
                act.activation(qk[:, :, :, 0:S], wide[:, 0].rearrange("p (k b s) -> p k b s", k=KC, b=B),
                               ACT.Copy).then_inc(qk_ready, 1)
                act.wait_ge(folded, 8)
                act.activation(wvT[:, :, C:CX], wide[:, 2, 16:16 + KC * EX].rearrange("p (k s) -> p k s", k=KC),
                               ACT.Copy).then_inc(wvT_ready, 1)
                act.activation(bv_ext[:, C:CX], wide[0:1, 2, 64:64 + EX], ACT.Copy).then_inc(wvT_ready, 1)

            def values():
                act.wait_ge(folded, 9)
                for b in range(2):
                    dst = v_sb[:, 0:B:2, :] if b == 0 else v_odd[S:P]
                    act.activation(dst, wide[b * S:(b + 1) * S, 0:B // 2, 0:CX], ACT.Copy).then_inc(v_ready, 1)

            def step(j):
                if active(j, 3):
                    g = j - 3
                    act.wait_ge(prb_turned, g + 1)
                    act.activation(prbT[:], bank[3][0:S, :], ACT.Copy).then_inc(prbT_ready, 1)
                if active(j, 1):
                    g = j - 1
                    for k in range(KC):
                        act.wait_ge(xc_turned, KC * g + k + 1)
                        act.activation(xcT[:, k], bank[k][:], ACT.Copy).then_inc(xcT_ready, 1)
                if active(j, 4):
                    g = j - 4
                    wait_count(act, squared, GT * g)
                    act.wait_ge(extra_ready, 3 * g + 3)
                    m, ss = columns_of(nm2, g), columns_of(ss2, g)
                    for i in range(GT):
                        act.wait_ge(x1_ready, GT * g + i + 1)
                        act.activation(sq[:, i, :], xcols(g)[:, i, :], ACT.Square, bias=m[:, i:i + 1],
                                       accum_out=ss[:, i:i + 1]).then_inc(squared, 1)
                if active(j, 2):
                    g = j - 2
                    act.wait_ge(max_ready, g + 1)
                    for i in range(GT):
                        a = act.activation(prb[:, i, :], score[:, i, :], ACT.Exp, bias=nmax[:, i:i + 1],
                                           accum_out=psums[:, i:i + 1])
                    a.then_inc(exp_done, 1)

            run_steps(act, step, {0: setup, 1: folded_keys, 2: values})

            act.wait_ge(soft, 3)
            pr = prob[:].rearrange("p b c e -> p (b c e)")
            act.activation(pr, pr, ACT.Exp).then_inc(gexp, 1)

            act.wait_ge(rows_stored, 16 * NG)
            act.wait_ge(nb2_ready, 1)
            with act.Fori(0, NG) as g:
                m, rs = columns_of(nb2, g), columns_of(rs2, g)
                for i in range(GT):
                    a = act.activation(xcols(g)[:, i, :], xcols(g)[:, i, :], ACT.Identity, bias=m[:, i:i + 1],
                                       scale=rs[:, i:i + 1])
                a.then_inc(xn2_ready, 1)

            act.activation(warm[:], neghalf[:, 0:1], ACT.Gelu)

            def w1_part(j, n):
                act.activation(w1hi[:, j], w1raw[:, :, bass.ts(j, P)], ACT.Copy).then_inc(w1_hi, 1)

            def w2_part(j, n):
                act.activation(w2hi[:, j], w2raw[:, j], ACT.Copy).then_inc(w2_hi, 1)

            act.wait_ge(raw_loaded, 32)
            for j in range(HC):
                w1_part(j, 0)
            for j in range(HC - 1):
                w2_part(j, 0)

            def x_part(g, k, n, src=2):
                act.wait_ge(xg_turned, n)
                act.activation(xhi[g][:, k], bank[src][:], ACT.Copy).then_inc(x_hi, 1)

            def gelu(s, n):
                act.wait_ge(ff1_done, n + 1)
                if not (isinstance(n, int) and n < 2):
                    act.wait_ge(h_split, n - 1)
                act.activation(hraw[s % 2][:], bank[s % 2][:], ACT.Gelu).then_inc(gelu_done, 1)

            def y_rows(g, e):
                act.wait_ge(pcol_ready, 2 * e + g + 1)
                if g == 0:
                    act.wait_ge(settled, e + 1)

                for i in range(NL):
                    if i % 2 == 0:
                        act.wait_ge(bank_done, (NL // 2) * (NU * e + g) + i // 2 + 1)
                    act.activation(ysb[g][:, i, :], bank[4 + 2 * g + i // 2][:, (i % 2) * C:(i % 2 + 1) * C],
                                       ACT.Copy, scale=pcol[g][:, i:i + 1]).then_inc(y_ready, 1)

            for k in range(KC):
                x_part(0, k, k + 1, 2 - k)
            gelu(0, 0)
            gelu(1, 1)

            def expert(e, last):
                for s in range(ST):
                    if s in (1, 2):
                        x_part(1, s - 1, 2 * NU * e + 2 + s)
                    if s in (10, 11) and not last:
                        x_part(0, s - 10, 2 * NU * (e + 1) + s - 9)
                    if s == 0:
                        act.wait_ge(ff1_done, ST * e + 2)
                        w2_part(HC - 1, 0)
                    if s == HC - 1 and not last:
                        act.wait_ge(raw_loaded, 32 * (e + 2))
                    if HC - 1 <= s < 2 * HC - 1 and not last:
                        j = s - (HC - 1)
                        act.wait_ge(ff1_done, ST * e + HC + j + 1)
                        w1_part(j, 0)
                    if s > HC and not last:
                        j = s - HC - 1
                        act.wait_ge(ff2_done, (HC - 1) * (NU * e + 1) + j + 1)
                        w2_part(j, 0)
                    if s + 2 < ST or not last:
                        gelu(s + 2, ST * e + s + 2)
                    if s % HC == HC - 1:
                        y_rows(s // HC, e)

            run_experts(act, expert)

        @block.tensor
        def _(pe):
            def turn(dst, src, ident=identf):
                return pe.transpose(dst, src, ident[:])

            pe.wait_ge(consts, N_CONST)
            pe.wait_ge(kv_loaded, 48)
            for dst, src in ((bank[0], ctx_sb), (bank[1], wk_sb)):
                for k in range(KC):
                    for r in range(2):
                        t = turn(dst[:, k * 256 + r * P:k * 256 + (r + 1) * P], src[:, r, k * P:(k + 1) * P])
                t.then_inc(folded, 1)
            pe.wait_ge(ctxT_ready, 1)
            pe.wait_ge(wkT_ready, 1)
            for m in range(KC):
                for k in range(KC):
                    t = pe.matmul((bank[3][:, 0:256], wide[:, 3, 0:256])[m], wkT[:, k, m * P:(m + 1) * P], ctxT[:, k, :],
                                  start=(k == 0), stop=(k == KC - 1))
            t.then_inc(folded, 1)
            pe.wait_ge(q_loaded, 48)
            for k in range(KC):
                t = pe.matmul(wide[:, 2, 0:E], inv_c[:], gate_sb[:, k, :], start=(k == 0), stop=(k == KC - 1))
            t.then_inc(folded, 1)
            pe.wait_ge(v_loaded, 48)
            for k in range(KC):
                for r in range(2):
                    t = turn(bank[2][:, k * 256 + r * P:k * 256 + (r + 1) * P], wv_sb[:, r, k * P:(k + 1) * P])
            t.then_inc(folded, 1)

            def folded_keys():
                pe.wait_ge(kT0_ready, 1)
                pe.wait_ge(kT1_ready, 1)
                for m in range(KC):
                    for k in range(KC):
                        t = pe.matmul(wide[:, 0, m * 256:(m + 1) * 256], wq_sb[:, k, m * P:(m + 1) * P], kT[:, k, :],
                                      start=(k == 0), stop=(k == KC - 1))
                t.then_inc(folded, 1)
                for k in range(KC):
                    t = pe.matmul(wide[:, 1, 0:B * S], bq_sb[:, k:k + 1].to_broadcast([P, P]), kT[:, k, :],
                                  start=(k == 0), stop=(k == KC - 1))
                t.then_inc(folded, 1)
                pe.wait_ge(gate_ready, KC)
                for r in range(KC):
                    for k in range(KC):
                        pe.matmul(wide[:, 2, 16 + r * EX:16 + (r + 1) * EX], wv_sb[:, k, r * P:(r + 1) * P],
                                  qk[:, k, 0, S:SX], start=(k == 0), stop=(k == KC - 1))
                for k in range(KC):
                    t = pe.matmul(wide[0:1, 2, 64:64 + EX], bv_col[:, k:k + 1], qk[:, k, 0, S:SX],
                                  start=(k == 0), stop=(k == KC - 1))
                t.then_inc(folded, 1)

            def values():
                pe.wait_ge(wvT_ready, 3)
                pe.wait_ge(qk_ready, 1)
                pe.wait_ge(qk_bias_ready, 1)
                for q in range(B // 2):
                    for k in range(KC):
                        pe.matmul(wide[:, q, 0:CX], ctxT[:, k, q * P:(q + 1) * P], wvT[:, k, :], start=(k == 0), stop=False)
                    t = pe.matmul(wide[:, q, 0:CX], ones_row[:], bv_ext[:], start=False, stop=True)
                t.then_inc(folded, 1)

            def keep_warm(dst, n):
                for _ in range(n):
                    turn(dst[:, 0:P], identf[:])

            def odd_values():
                pe.wait_ge(v_moved, 16)

            def step(j):
                if active(j, 2):
                    g = j - 2
                    pe.wait_ge(xcT_ready, KC * (g + 1))
                    if isinstance(g, int) and g == 0:
                        pe.wait_ge(qk_ready, 1)
                    wait_count(pe, max_ready, g)
                    for i in range(GT):
                        for k in range(KC):
                            t = pe.matmul(bank[2][:, i * SX:(i + 1) * SX], xcT[:, k, i * P:(i + 1) * P],
                                          qk[:, k, bass.ds(g // GB, 1), :], start=(k == 0), stop=(k == KC - 1))
                    t.then_inc(scored, 1)
                if active(j, 3):
                    g = j - 3
                    if isinstance(g, int) and g == NG - 1:
                        keep_warm(bank[0], 8)
                    pe.wait_ge(exp_done, g + 1)
                    wait_count(pe, prbT_ready, g)
                    keep_wait(pe, pe_passed)
                    for i in range(GT):
                        t = turn(bank[3][0:S, i * P:(i + 1) * P], prb[:, i, :])
                    t.then_inc(prb_turned, 1)
                    if isinstance(g, int) and g == NG - 1:
                        keep_warm(bank[0], 6)
                if active(j, 1):
                    g = j - 1
                    pe.wait_ge(xc_ready, g + 1)
                    wait_count(pe, xcT_ready, KC * g)
                    for k in range(KC):
                        for i in range(GT):
                            t = turn(bank[k][:, i * P:(i + 1) * P], xc[:, i, k * P:(k + 1) * P])
                        t.then_inc(xc_turned, 1)
                if active(j, 3):
                    g = j - 3
                    if isinstance(g, int) and g == 0:
                        pe.wait_ge(v_ready, 2)
                    pe.wait_ge(prbT_ready, g + 1)
                    wait_count(pe, x1_ready, GT * g)
                    for i in range(GT):
                        t = pe.matmul(wide[:, i, 0:CX], prbT[:, i * P:(i + 1) * P],
                                      v_sb[:, bass.ds(g // GB, 1), :], start=True, stop=True)
                    t.then_inc(attended, 1)

            run_steps(pe, step, {1: folded_keys, 2: values, 4: odd_values})

            with pe.Fori(0, 2 * ROUNDS) as r:
                for h in range(2):
                    for b in range(HB):
                        pe.wait_ge(over_ready[h][b], r + 1)
                        for c in range(TC):
                            t = pe.matmul(counts(h)[:, b, E:], onesb[:], over[:, h * HB + b, c, :],
                                          start=(c == 0), stop=(c == TC - 1))
                    t.then_inc(counted[h], 1)
            def rank_bases(h):
                pe.wait_ge(summed[h], 2)
                sums = upto[h][:].rearrange("p m b e c -> p (m b e) c")[:, :, TC - 1]
                o = bank[2 + 2 * h]
                pe.matmul(o[:, 0:2 * HB * E], before[:], sums, start=True, stop=False, skip_group_check=True)
                pe.matmul(o[:, HB * E:2 * HB * E], onesb[:], sums[:, 0:HB * E], start=False, stop=True,
                          skip_group_check=True).then_inc(ranked[h], 1)

            def list_batch(b, e, dst=3):
                pe.wait_ge(onehot_ready[b], e + 1)
                for c in range(TC):
                    t = pe.matmul(bank[dst][:, b * LB:(b + 1) * LB], onehot[:, b, :, c],
                                  tok_val[:, b, bass.ds(e, 1), :, c].rearrange("p e l -> p (e l)"),
                                  start=(c == 0), stop=(c == TC - 1))
                t.then_inc(listed[b // UB], 1)

            def turn_rows(g, k, n, src=None):
                if src is None:
                    pe.wait_ge(x_split, n)
                for i in range(NL):
                    t = turn(bank[src or 2][:, i * P:(i + 1) * P], xg[g][:, i, k * P:(k + 1) * P])
                t.then_inc(xg_turned, 1)

            def ff1(s, n, e):
                g, j = s // HC, s % HC
                if j == 0:
                    pe.wait_ge(x_hi, 2 * NU * e + 2 * (g + 1))
                if g == 0:
                    pe.wait_ge(w1_split, HC * e + j + 1)
                if not (isinstance(n, int) and n < 2):
                    pe.wait_ge(gelu_done, n - 1)
                m = 0
                for w, xx in ((w1hi, xhi), (w1lo, xhi), (w1hi, xlo)):
                    if j == 0 and xx is xlo:
                        pe.wait_ge(x_split, 2 * NU * e + 2 * (g + 1))
                    for k in range(KC):
                        t = pe.matmul(bank[s % 2][:], w[:, j, k, :], xx[g][:, k, :], start=(m == 0), stop=(m == 5))
                        m += 1
                t.then_inc(ff1_done, 1)

            def ff2(s, n, e):
                g, j = s // HC, s % HC
                if g == 0:
                    pe.wait_ge(w2_split, HC * e + j + 1)
                pe.wait_ge(h_split, n + 1)
                for i in range(NL):
                    o = bank[4 + 2 * g + i // 2][:, (i % 2) * C:(i % 2 + 1) * C]
                    for m, (hh, w) in enumerate(((hhi, w2hi), (hhi, w2lo), (hlo, w2hi))):
                        t = pe.matmul(o, hh[s % 4][:, i * P:(i + 1) * P], w[:, j, :],
                                      start=(j == 0 and m == 0 and i % 2 == 0), stop=(j == HC - 1 and m == 2),
                                      skip_group_check=True)
                    if j == HC - 1 and i % 2 == 1:
                        t.then_inc(bank_done, 1)
                if j < HC - 1:
                    t.then_inc(ff2_done, 1)

            for g in range(NU):
                rank_bases(g)
                if g == 1:
                    keep_warm(wide[:, 3], 20)
                for b in range(g * UB, (g + 1) * UB):
                    list_batch(b, 0, 3 if b < UB else 0)
            pe.wait_ge(gathered[0], 16 * NL)
            for k in range(KC):
                turn_rows(0, k, k, src=2 - k)
            keep_warm(wide[:, 3], 6)
            pe.wait_ge(gidx_ready[1], 1)
            ff1(0, 0, 0)
            ff1(1, 1, 0)

            def expert(e, last):
                for s in range(ST):
                    if s + 2 < ST:
                        ff1(s + 2, ST * e + s + 2, e)
                    elif not last:
                        ff1(s + 2 - ST, ST * e + s + 2, e + 1)
                    if s == 1:
                        pe.wait_ge(gathered[1], 16 * NL * (e + 1))
                    if s in (1, 2):
                        turn_rows(1, s - 1, 2 * NU * e + 1 + s)
                    if s == 10 and not last:
                        pe.wait_ge(gathered[0], 16 * NL * (e + 2))
                    if s in (10, 11) and not last:
                        turn_rows(0, s - 10, 2 * NU * (e + 1) + s - 10)
                    if 1 <= s <= B and not last:
                        list_batch(s - 1, e + 1)
                    ff2(s, ST * e + s, e)

            run_experts(pe, expert)

        @block.vector
        def _(dve):
            dve.wait_ge(consts, N_CONST)
            for r in range(ROUNDS):
                dve.tensor_scalar(step_wide[:, r], step_wide[:, r], BITS - RB * (r + 1), None,
                                  ALU.logical_shift_left).then_inc(bits_ready, 1)
            dve.wait_ge(bits_ready, ROUNDS)
            dve.tensor_copy(step_bits[:], step_wide[:]).then_inc(bits_ready, 1)
            dve.wait_ge(folded, 2)
            dve.tensor_copy(wkT[:].rearrange("p k s -> p (k s)"), bank[1][:]).then_inc(wkT_ready, 1)

            def setup():
                dve.wait_ge(folded, 3)
                dve.tensor_scalar(kT[:, 1], wide[:, 3, 0:256], bk_sb[:, 1:2], None, ALU.add).then_inc(kT1_ready, 1)
                dve.wait_ge(folded, 4)
                for k in range(KC):
                    dve.tensor_tensor(qk[:, k, :, S:S + E], gate_sb[:, k].unsqueeze(1).to_broadcast([P, B, E]),
                                      wide[:, 2, 0:E].unsqueeze(1).to_broadcast([P, B, E]),
                                      ALU.subtract).then_inc(gate_ready, 1)

            def bias():
                dve.wait_ge(folded, 7)
                dve.tensor_copy(qk_bias[:].rearrange("p b s -> p (b s)"), wide[:, 1, 0:B * S]).then_inc(qk_bias_ready, 1)

            def step(j):
                if isinstance(j, int) and j < 3:
                    dve.wait_ge((x_first, x_second, x_rest)[j], 16 * (1, 1, B - 1)[j])
                if active(j, 4):
                    g = j - 4
                    xcg, ex = xcols(g), columns_of(extra, g)

                    def residual(i):
                        dve.scalar_tensor_tensor(out=xcg[:, i, :], in0=wide[:, i, 0:C], scalar=rinv[:, i:i + 1],
                                                 in1=xcg[:, i, :], op0=ALU.mult, op1=ALU.add).then_inc(x1_ready, 1)

                    dve.wait_ge(attended, g + 1)
                    dve.wait_ge(rinv_ready, g + 1)
                    dve.tensor_tensor(extra_v[:], wide[:, :, C:CX], rinv[:].unsqueeze(2).to_broadcast([P, GT, EX]),
                                      ALU.mult).then_inc(extra_ready, 1)
                    residual(0)
                    dve.wait_ge(extra_ready, 3 * g + 1)
                    dve.tensor_tensor(ex, ex, extra_v[:], ALU.add).then_inc(extra_ready, 1)
                    residual(1)
                    dve.wait_ge(extra_ready, 3 * g + 2)
                    dve.scalar_tensor_tensor(out=columns_of(nm2, g).unsqueeze(2), in0=ex[:, :, E:EX], scalar=-1.0,
                                             in1=columns_of(nm1, g).unsqueeze(2),
                                             op0=ALU.mult, op1=ALU.add).then_inc(extra_ready, 1)
                    residual(2)
                    residual(3)
                if active(j, 0):
                    g = j
                    keep_wait(dve, dve_passed)
                    for i in range(GT):
                        t = dve.bn_stats(st1[:, i, :], xcols(g)[:, i, :])
                    t.then_inc(stats1, 1)
                if active(j, 2):
                    g = j - 2
                    dve.wait_ge(rstd1, g + 1)
                    dve.wait_ge(scored, g + 1)
                    wait_count(dve, exp_done, g)
                    if isinstance(g, int) and g == 0:
                        dve.wait_ge(qk_bias_ready, 1)
                    for i in range(GT):
                        t = dve.scalar_tensor_tensor(out=score[:, i, :], in0=bank[2][:, i * SX:i * SX + S],
                                                     scalar=columns_of(rs1, g)[:, i:i + 1],
                                                     in1=qk_bias[:, bass.ds(g // GB, 1), :].rearrange("p b s -> p (b s)"),
                                                     op0=ALU.mult, op1=ALU.add)
                    t.then_inc(score_ready, 1)
                    dve.tensor_copy(columns_of(extra, g),
                                    bank[2][:, 0:GT * SX].rearrange("p (i s) -> p i s", i=GT)[:, :, S:SX])
                if active(j, 3):
                    g = j - 3
                    dve.wait_ge(exp_done, g + 1)
                    wait_count(dve, x1_ready, GT * g)
                    dve.reciprocal(rinv[:], psums[:]).then_inc(rinv_ready, 1)
                if active(j, 0):
                    g = j
                    dve.wait_ge(stats1, 2 * g + 1)
                    keep_wait(dve, dve_passed)
                    for i in range(GT):
                        t = dve.bn_aggr(mv1[:, i, :], st1[:, i, :])
                    t.then_inc(stats1, 1)
                if active(j, 2):
                    g = j - 2
                    dve.wait_ge(score_ready, g + 1)
                    dve.tensor_reduce(nmax[:], score[:], AX.X, ALU.max, negate=True).then_inc(max_ready, 1)
                if active(j, 0):
                    g = j
                    dve.wait_ge(stats1, 2 * g + 2)
                    dve.tensor_scalar(columns_of(nm1, g), mv1[:, :, 0], -1.0, None, ALU.mult).then_inc(mean1, 1)
                    dve.tensor_scalar(columns_of(ve1, g), mv1[:, :, 1], EPS, None, ALU.add).then_inc(var1, 1)

            def variances(lo, hi):
                dve.wait_ge(squared, hi)
                dve.tensor_scalar(ve2[:, lo:hi], ss2[:, lo:hi], 1.0 / C, EPS, ALU.mult, ALU.add).then_inc(ve2_ready, 1)

            run_steps(dve, step, {0: setup, 1: bias, NG + 1: lambda: variances(0, NC - 3 * GT),
                                  NG + 2: lambda: variances(NC - 3 * GT, NC - GT)})
            variances(NC - GT, NC)

            logits = extra[:, :, 0:E]
            pr = prob[:].rearrange("p b c e -> p (b c) e")
            dve.wait_ge(rstd2, 3)
            dve.tensor_tensor(logits, logits, rs2[:].unsqueeze(2).to_broadcast([P, NC, E]), ALU.mult).then_inc(soft, 1)
            dve.wait_ge(soft, 1)
            dve.tensor_reduce(gmax[:], logits, AX.X, ALU.max).then_inc(soft, 1)
            dve.wait_ge(soft, 2)
            dve.tensor_tensor(pr, logits, gmax[:].unsqueeze(2).to_broadcast([P, NC, E]), ALU.subtract).then_inc(soft, 1)
            dve.tensor_tensor(nb2[:], nm2[:], rs2[:], ALU.mult).then_inc(nb2_ready, 1)
            dve.wait_ge(gexp, 1)
            dve.tensor_reduce(gsum[:], pr, AX.X, ALU.add).then_inc(soft, 1)
            dve.wait_ge(soft, 4)
            dve.reciprocal(gmax[:], gsum[:]).then_inc(soft, 1)
            dve.wait_ge(soft, 5)
            dve.tensor_tensor(pr, pr, gmax[:].unsqueeze(2).to_broadcast([P, NC, E]), ALU.mult).then_inc(soft, 1)


            def flat(ap):
                return ap.rearrange("p b c e -> p (b c e)")

            def try_bits(h, r, n):
                full = [P, HB, KT + 1, E]
                dve.tensor_tensor(half(cand, h), half(floor_, h).unsqueeze(2).to_broadcast(full),
                                  step_bits[:, bass.ds(r, 1)].to_broadcast(full), ALU.bitwise_or).then_inc(cand_ready[h], 1)

            def compare(h, b, n):
                dve.wait_ge(cand_ready[h], n + 1)
                dve.tensor_tensor(
                    half(over, h)[:, b].rearrange("p c (k e) -> p c k e", k=KT),
                    half(key, h)[:, b].unsqueeze(2).to_broadcast([P, TC, KT, E]),
                    half(cand, h)[:, b, 1:].unsqueeze(1).to_broadcast([P, TC, KT, E]), ALU.is_ge).then_inc(over_ready[h][b], 1)

            def keep_reached(h, n):
                dve.wait_ge(counted[h], n + 1)
                dve.scalar_tensor_tensor(out=half(reached, h).rearrange("p b k e -> p b (k e)"), in0=counts(h),
                                         scalar=float(CAP), in1=half(cand, h).rearrange("p b k e -> p b (k e)"),
                                         op0=ALU.is_ge, op1=ALU.mult).then_inc(reached_ready[h], 1)

            def raise_floor(h, n):
                dve.wait_ge(reached_ready[h], n + 1)
                dve.tensor_reduce(half(floor_, h), half(reached, h).rearrange("p b k e -> p b e k"), AX.X,
                                  ALU.max).then_inc(floor_ready[h], 1)

            def half_round(h, r, n, n_other):
                keep_reached(h, n)
                compare(1 - h, HB - 1, n_other)
                raise_floor(h, n)
                dve.wait_ge(floor_ready[h], n + 1)
                try_bits(h, r + 1, n + 1)
                for b in range(HB - 1):
                    compare(h, b, n + 1)

            def bisect(n0):
                try_bits(0, 0, n0)
                try_bits(1, 0, n0)
                for b in range(HB):
                    compare(0, b, n0)
                for b in range(HB - 1):
                    compare(1, b, n0)
                UR = 2
                assert (ROUNDS - 1) % UR == 0
                with dve.Fori(0, (ROUNDS - 1) // UR) as q:
                    for i in range(UR):
                        r = q * UR + i
                        half_round(0, r, n0 + r, n0 + r)
                        half_round(1, r, n0 + r, n0 + r + 1)
                last = n0 + ROUNDS - 1
                keep_reached(0, last)
                compare(1, HB - 1, last)
                raise_floor(0, last)
                dve.wait_ge(floor_ready[0], last + 1)

            def end_half_1(last):
                keep_reached(1, last)
                raise_floor(1, last)
                dve.wait_ge(floor_ready[1], last + 1)

            dve.wait_ge(soft, 6)
            dve.tensor_scalar(flat(upper[:]), flat(prob[:].bitcast(I32)), BITS, None,
                              ALU.logical_shift_right).then_inc(key_parts, 1)
            dve.tensor_scalar(flat(lower[:]), flat(prob[:].bitcast(I32)), 2 ** BITS - 1, None,
                              ALU.bitwise_and).then_inc(key_parts, 1)
            for h in range(2):
                dve.memset(counts(h)[:, :, 0:E], float(T))
            dve.wait_ge(bits_ready, ROUNDS + 1)
            dve.wait_ge(key_parts, 1)
            dve.tensor_copy(flat(key[:]), flat(upper[:])).then_inc(key_ready, 1)
            dve.wait_ge(key_ready, 1)
            bisect(0)
            end_half_1(ROUNDS - 1)

            for h in range(2):
                dve.tensor_copy(half(found, h), half(floor_, h)).then_inc(found_ready[h], 1)
            for b in range(B):
                t = dve.tensor_tensor(above_found[:, b], upper[:, b], floor_[:, b].unsqueeze(1).to_broadcast([P, TC, E]),
                                      ALU.subtract)
            t.then_inc(key_parts, 1)
            for h in range(2):
                dve.wait_ge(found_ready[h], 1)
                dve.tensor_scalar(half(found, h), half(found, h), BITS, None,
                                  ALU.logical_shift_left).then_inc(found_ready[h], 1)
            dve.wait_ge(key_parts, 3)
            dve.scalar_tensor_tensor(out=flat(above_found[:]), in0=flat(above_found[:]), scalar=float(2 ** BITS),
                                     in1=flat(lower[:]), op0=ALU.mult, op1=ALU.add).then_inc(key_parts, 1)
            dve.memset(floor_[:], 0)
            dve.wait_ge(key_parts, 4)
            dve.tensor_scalar(flat(key[:]), flat(above_found[:]), float(2 ** BITS - 1), -1.0, ALU.min,
                              ALU.max).then_inc(key_ready, 1)
            dve.wait_ge(key_ready, 2)
            bisect(ROUNDS)

            def place_chosen(h):
                dve.tensor_copy(half(last_bits, h), half(floor_, h)).then_inc(found_ready[h], 1)
                dve.wait_ge(found_ready[h], 3)
                dve.tensor_tensor(half(found, h), half(found, h), half(last_bits, h),
                                  ALU.bitwise_or).then_inc(found_ready[h], 1)
                dve.wait_ge(found_ready[h], 4)
                for m, op in ((0, ALU.is_gt), (1, ALU.is_equal)):
                    dve.tensor_tensor(mask[h][:, m], half(prob, h).rearrange("p b c e -> p b e c"),
                                      half(found, h).bitcast(F32).unsqueeze(3).to_broadcast([P, HB, E, TC]),
                                      op).then_inc(masks[h], 1)

                def flat(ap):
                    return ap.rearrange("p b e c -> p (b e c)")

                for m in range(2):
                    dve.wait_ge(masks[h], m + 1)
                    dve.tensor_tensor_scan(flat(upto[h][:, m]), flat(go_on[:]), flat(mask[h][:, m]), 0.0, ALU.mult,
                                           ALU.add).then_inc(summed[h], 1)
                dve.wait_ge(summed[h], 2)
                dve.wait_ge(ranked[h], 1)
                dve.tensor_tensor(place[h][:].rearrange("p m b e c -> p (m b e) c"),
                                  upto[h][:].rearrange("p m b e c -> p (m b e) c"),
                                  bank[2 + 2 * h][:, 0:2 * HB * E].unsqueeze(2).to_broadcast([P, 2 * HB * E, TC]),
                                  ALU.add).then_inc(placed[h], 1)
                dve.wait_ge(placed[h], 1)
                dve.tensor_tensor(place[h][:].rearrange("p m b e c -> p (m b e c)"),
                                  place[h][:].rearrange("p m b e c -> p (m b e c)"),
                                  mask[h][:].rearrange("p m b e c -> p (m b e c)"), ALU.mult).then_inc(placed[h], 1)
                dve.wait_ge(placed[h], 2)
                dve.tensor_tensor(flat(half(slot_any, h)), flat(place[h][:, 0]), flat(place[h][:, 1]),
                                  ALU.add).then_inc(placed[h], 1)
                dve.wait_ge(placed[h], 3)
                dve.tensor_scalar(flat(half(second, h)), flat(half(slot_any, h)), P + 0.5, None,
                                  ALU.is_gt).then_inc(placed[h], 1)
                dve.wait_ge(placed[h], 4)
                dve.scalar_tensor_tensor(out=flat(half(slot_of, h)), in0=flat(half(second, h)), scalar=-float(P),
                                         in1=flat(half(slot_any, h)), op0=ALU.mult, op1=ALU.add).then_inc(placed[h], 1)
                tv = half(tok_val, h).rearrange("p b e l c -> p (b e) l c")
                tn = half(tok_no, h).rearrange("p b e c -> p (b e) c")
                dve.tensor_tensor(tv[:, :, 1, :], half(second, h).rearrange("p b e c -> p (b e) c"), tn,
                                  ALU.mult).then_inc(placed[h], 1)
                dve.wait_ge(placed[h], 6)
                dve.tensor_tensor(tv[:, :, 0, :], tn, tv[:, :, 1, :], ALU.subtract).then_inc(placed[h], 1)
                dve.wait_ge(placed[h], 7)

            def one_hot(b, e):
                dve.tensor_tensor(onehot[:, b], slot_no[:], slot_of[:, b, bass.ds(e, 1), :].to_broadcast([P, P, TC]),
                                  ALU.is_equal).then_inc(onehot_ready[b], 1)

            def index_list(g, e, src=3):
                dve.wait_ge(listed[g], UB * (e + 1))
                dve.tensor_tensor(gidx[:, g * NL:(g + 1) * NL], bank[src][:, g * NL:(g + 1) * NL],
                                  row0[:, g * NL:(g + 1) * NL], ALU.add).then_inc(gidx_ready[g], 1)

            def x_rest_part(g, k, n, src=2):
                dve.wait_ge(x_hi, n)
                dve.tensor_tensor(xlo[g][:, k], bank[src][:], xhi[g][:, k].bitcast(F32), ALU.subtract).then_inc(x_split, 1)

            def prob_column(g, e):
                dve.tensor_copy(pcol[g][:].unsqueeze(2), pg[g][:, :, bass.ds(e, 1)]).then_inc(pcol_ready, 1)

            def split_h(s, n):
                dve.wait_ge(gelu_done, n + 1)
                dve.tensor_copy(hhi[s % 4][:], hraw[s % 2][:]).then_inc(h_hi, 1)
                dve.wait_ge(h_hi, n + 1)
                dve.tensor_tensor(hlo[s % 4][:], hraw[s % 2][:], hhi[s % 4][:].bitcast(F32),
                                  ALU.subtract).then_inc(h_split, 1)

            dve.wait_ge(first_split, 2 * HC - 1)
            dve.sem_inc(w1_split, HC)
            dve.sem_inc(w2_split, HC - 1)

            for g in range(NU):
                if g == 1:
                    end_half_1(2 * ROUNDS - 1)
                place_chosen(g)
                for b in range(g * UB, (g + 1) * UB):
                    one_hot(b, 0)
                index_list(g, 0, 3 if g == 0 else 0)
            for k in range(KC):
                x_rest_part(0, k, k + 1, 2 - k)
            split_h(0, 0)
            split_h(1, 1)

            def expert(e, last):
                for s in range(ST):
                    if s == 0:
                        dve.wait_ge(w2_hi, HC * (e + 1))
                        dve.tensor_tensor(w2lo[:, HC - 1], w2raw[:, HC - 1], w2hi[:, HC - 1].bitcast(F32),
                                          ALU.subtract).then_inc(w2_split, 1)
                    if s in (1, 2):
                        x_rest_part(1, s - 1, 2 * NU * e + 2 + s)
                    if s == 3:
                        dve.wait_ge(prob_gathered[0], 16 * NL * (e + 1))
                        prob_column(0, e)
                    if s == 5:
                        dve.wait_ge(prob_gathered[1], 16 * NL * (e + 1))
                        prob_column(1, e)
                    if s < B and not last:
                        one_hot(s, e + 1)
                    if s == 4:
                        dve.wait_ge(settled, e + 1)
                        dve.tensor_copy(sidx[:], gidx[:]).then_inc(sidx_ready, 1)
                    if s == 6 and not last:
                        dve.wait_ge(sidx_ready, e + 1)
                        for g in range(NU):
                            index_list(g, e + 1)
                    if s in (10, 11) and not last:
                        x_rest_part(0, s - 10, 2 * NU * (e + 1) + s - 9)
                    if s == 11 and not last:
                        dve.wait_ge(y_ready, NL * (NU * e + 1))
                    if HC - 1 <= s < 2 * HC - 1 and not last:
                        j = s - (HC - 1)
                        dve.wait_ge(w1_hi, HC * (e + 1) + j + 1)
                        dve.tensor_tensor(w1lo[:, j], w1raw[:, :, bass.ts(j, P)], w1hi[:, j].bitcast(F32),
                                          ALU.subtract).then_inc(w1_split, 1)
                    if s > HC and not last:
                        j = s - HC - 1
                        dve.wait_ge(w2_hi, HC * (e + 1) + j + 1)
                        dve.tensor_tensor(w2lo[:, j], w2raw[:, j], w2hi[:, j].bitcast(F32),
                                          ALU.subtract).then_inc(w2_split, 1)
                    if s + 2 < ST or not last:
                        split_h(s + 2, ST * e + s + 2)

            run_experts(dve, expert)


_INS = ['x', 'ctx_1024', 'L0_xattn_Wq', 'L0_xattn_bq', 'L0_xattn_Wk', 'L0_xattn_bk', 'L0_xattn_Wv', 'L0_xattn_bv',
        'L0_ffn_gate_w', 'L0_ffn_w1', 'L0_ffn_w2']


def kernel(**inputs):
    import numpy as _np
    import concourse.bacc as _bacc
    from concourse import mybir as _mybir
    from concourse.bass_utils import run_bass_kernel_spmd as _run

    nc = _bacc.Bacc("TRN2", target_bir_lowering=False, num_devices=1)
    arrays, args = {}, []
    for name in _INS:
        a = _np.ascontiguousarray(inputs[name])
        arrays[f"in_{name}_dram"] = a
        args.append(nc.dram_tensor(f"in_{name}_dram", a.shape, _mybir.dt.from_np(a.dtype), kind="ExternalInput").ap())
    args.append(nc.dram_tensor("out_0_dram", inputs['x'].shape, _mybir.dt.float32, kind="ExternalOutput").ap())
    build(nc, *args)
    r = _run(nc, [arrays], core_ids=[0])
    return r.results[0]["out_0_dram"]
```
